# Optimizing a Trainium2 kernel written in Bass

```python
import numpy as np
import jax
import jax.numpy as jnp

def _softmax(x, axis=-1):
    return jax.nn.softmax(x, axis=axis)

def _gelu(x):
    return jax.nn.gelu(x, approximate=True)

def _silu(x):
    return jax.nn.silu(x)

def _sigmoid(x):
    return jax.nn.sigmoid(x)

def _layernorm(x, axis=-1, eps=1e-05):
    m = jnp.mean(x, axis=axis, keepdims=True)
    v = jnp.var(x, axis=axis, keepdims=True)
    return (x - m) / jnp.sqrt(v + eps)

def _scatter_add(tgt, idx, src, axis=0):
    return tgt.at[idx].add(src)

def _segment_sum(src, seg, n):
    return jax.ops.segment_sum(src, seg, n)
kernel_name = 'mk_adj_resnorm_d4_adj_r2_ca4e2f'

def setup_inputs(seed: int=0):
    np.random.seed(seed)
    _w = jnp.asarray

    def _rec_inputs():
        import jax
        import jax.numpy as jnp
        _gk = jax.random.key(seed)
        x = -0.0002928 + 1 * jax.random.normal(jax.random.fold_in(_gk, 1), (1354, 256), jnp.float32)
        _w = (1.0 + jnp.arange(1354, dtype=jnp.float32)) ** (-0.5)
        _w = _w / _w.mean()
        _pij = jnp.clip(0.0118168 * _w[:, None] * _w[None, :], 0.0, 1.0)
        _a = jax.random.uniform(jax.random.fold_in(_gk, 2), (1354, 1354)) < _pij
        _a = jnp.logical_or(_a, jnp.eye(1354, dtype=bool))
        _af = _a.astype(jnp.float32)
        _af = _af * jax.random.uniform(jax.random.fold_in(_gk, 3), (1354, 1354), jnp.float32, 0.05, 1)
        adj = _af
        return (x, adj)
    x, adj = _rec_inputs()

    def _L0_gnn_setup():
        import jax, jax.numpy as jnp
        import numpy as np

        def _bin_sign(v):
            return jnp.sign(v)

        def _bin_sign_z(v):
            return jnp.maximum(jnp.sign(v), 0.0)
        key = jax.random.key(seed)
        k1, k2, k3 = jax.random.split(key, 3)
        N, D_IN, D_OUT = (4096, 256, 256)
        x = jax.random.normal(k1, (N, D_IN), dtype=jnp.float32)
        support = jax.random.uniform(k2, (N, N), dtype=jnp.float32)
        weight = jax.random.normal(k3, (D_OUT, D_IN), dtype=jnp.float32)
        return {'x': x, 'support': support, 'weight': weight}
    _L0_gnn_all = _L0_gnn_setup()
    _L0_gnn_in = {k: v for k, v in _L0_gnn_all.items() if k in ('weight',)}
    del _L0_gnn_all

    def _L1_gnn_setup():
        import jax, jax.numpy as jnp
        import numpy as np
        N = 3072
        D_IN = 256
        D_OUT = 256
        DENSITY = 0.005
        key = jax.random.key(seed)
        ks = jax.random.split(key, 12)
        x = jax.random.normal(ks[0], (N, D_IN), dtype=jnp.float32)
        adj_a = (jax.random.uniform(ks[1], (N, N)) < DENSITY).astype(jnp.float32)
        adj_b = (jax.random.uniform(ks[2], (N, N)) < DENSITY).astype(jnp.float32)
        W_sa = jax.random.normal(ks[3], (D_IN, D_OUT), dtype=jnp.float32) * (1.414 / np.sqrt(D_IN + D_OUT))
        a_sa = jax.random.normal(ks[4], (1, 2 * D_OUT), dtype=jnp.float32) * (1.414 / np.sqrt(1 + 2 * D_OUT))
        stdv = 1.0 / np.sqrt(D_OUT)
        W_gcnb = jax.random.uniform(ks[5], (D_IN, D_OUT), minval=-stdv, maxval=stdv, dtype=jnp.float32)
        b_gcnb = jax.random.uniform(ks[6], (D_OUT,), minval=-stdv, maxval=stdv, dtype=jnp.float32)
        s = 1.0 / np.sqrt(2 * D_IN)
        Wa = jax.random.uniform(ks[7], (1, 2 * D_IN), minval=-s, maxval=s, dtype=jnp.float32)
        ba = jax.random.uniform(ks[8], (1,), minval=-s, maxval=s, dtype=jnp.float32)
        Wb = jax.random.uniform(ks[9], (1, 2 * D_IN), minval=-s, maxval=s, dtype=jnp.float32)
        bb = jax.random.uniform(ks[10], (1,), minval=-s, maxval=s, dtype=jnp.float32)
        return {'x': x, 'adj_a': adj_a, 'adj_b': adj_b, 'W_sa': W_sa, 'a_sa': a_sa, 'W_gcnb': W_gcnb, 'b_gcnb': b_gcnb, 'Wa': Wa, 'ba': ba, 'Wb': Wb, 'bb': bb}
    _L1_gnn_all = _L1_gnn_setup()
    _L1_gnn_in = {k: v for k, v in _L1_gnn_all.items() if k in ('W_sa', 'a_sa', 'W_gcnb', 'b_gcnb', 'Wa', 'ba', 'Wb', 'bb')}
    del _L1_gnn_all

    def _L2_gnn_setup():
        import jax, jax.numpy as jnp
        import numpy as np
        N = 4096
        F_IN = 256
        F_OUT = 256
        DENSITY = 0.01
        key = jax.random.key(seed)
        k_x, k_adj, k_w, k_b = jax.random.split(key, 4)
        input_features = jax.random.normal(k_x, (N, F_IN), dtype=jnp.float32)
        adj = (jax.random.uniform(k_adj, (N, N)) < DENSITY).astype(jnp.float32)
        idx = jnp.arange(N)
        adj = adj.at[idx, idx].set(1.0)
        W = jax.random.normal(k_w, (F_IN, F_OUT), dtype=jnp.float32) / np.sqrt(F_IN)
        b = jax.random.normal(k_b, (F_OUT,), dtype=jnp.float32) * 0.01
        return {'input_features': input_features, 'adj': adj, 'W': W, 'b': b}
    _L2_gnn_all = _L2_gnn_setup()
    _L2_gnn_in = {k: v for k, v in _L2_gnn_all.items() if k in ('W', 'b')}
    del _L2_gnn_all

    def _L3_gnn_setup():
        import jax, jax.numpy as jnp
        import numpy as np
        N = 4096
        D = 256
        L = 2
        NEG_SLOPE = 0.01

        def _gat_layer(x, W, adj):
            proj = x @ W
            Wh, Ws = jnp.split(proj, 2, axis=-1)
            scores = Wh @ Ws.T
            a = jax.nn.softmax(scores, axis=-1) * adj
            out = a @ Wh
            out = out + x
            return jax.nn.leaky_relu(out, NEG_SLOPE)
        key = jax.random.key(seed)
        k1, k2, k3 = jax.random.split(key, 3)
        inputs = jax.random.normal(k1, (N, D), dtype=jnp.float32)
        adj = jax.random.randint(k2, (N, N), 0, 2).astype(jnp.float32)
        W_stack = jax.random.normal(k3, (L, D, 2 * D), dtype=jnp.float32) * (1.0 / np.sqrt(D))
        return {'inputs': inputs, 'adj': adj, 'W_stack': W_stack}
    _L3_gnn_all = _L3_gnn_setup()
    _L3_gnn_in = {k: v for k, v in _L3_gnn_all.items() if k in ('W_stack',)}
    del _L3_gnn_all
    return {'x': x, 'adj': adj, 'L0_gnn_weight': _L0_gnn_in['weight'], 'L1_gnn_W_sa': _L1_gnn_in['W_sa'], 'L1_gnn_a_sa': _L1_gnn_in['a_sa'], 'L1_gnn_W_gcnb': _L1_gnn_in['W_gcnb'], 'L1_gnn_b_gcnb': _L1_gnn_in['b_gcnb'], 'L1_gnn_Wa': _L1_gnn_in['Wa'], 'L1_gnn_ba': _L1_gnn_in['ba'], 'L1_gnn_Wb': _L1_gnn_in['Wb'], 'L1_gnn_bb': _L1_gnn_in['bb'], 'L2_gnn_W': _L2_gnn_in['W'], 'L2_gnn_b': _L2_gnn_in['b'], 'L3_gnn_W_stack': _L3_gnn_in['W_stack']}

def reference(x, adj, L0_gnn_weight, L1_gnn_W_sa, L1_gnn_a_sa, L1_gnn_W_gcnb, L1_gnn_b_gcnb, L1_gnn_Wa, L1_gnn_ba, L1_gnn_Wb, L1_gnn_bb, L2_gnn_W, L2_gnn_b, L3_gnn_W_stack):
    import jax
    import jax.numpy as jnp

    def _L0_gnn_ref(x, support, weight):
        import jax, jax.numpy as jnp
        import numpy as np

        def _bin_sign(v):
            return jnp.sign(v)

        def _bin_sign_z(v):
            return jnp.maximum(jnp.sign(v), 0.0)
        bw = _bin_sign(weight)
        ba = _bin_sign_z(x)
        xw = ba @ bw.T
        out = support @ xw
        return jax.nn.relu(out)

    def _L1_gnn_ref(x, adj_a, adj_b, W_sa, a_sa, W_gcnb, b_gcnb, Wa, ba, Wb, bb):
        import jax, jax.numpy as jnp
        import numpy as np
        N = 3072
        D_IN = 256
        D_OUT = 256
        DENSITY = 0.005
        type_sum_a = adj_a @ x
        type_sum_b = adj_b @ x
        attn_a = jax.nn.sigmoid(jnp.concatenate([type_sum_a, x], axis=1) @ Wa.T + ba)
        attn_b = jax.nn.sigmoid(jnp.concatenate([type_sum_b, x], axis=1) @ Wb.T + bb)
        h = x @ W_sa
        Hd = h.shape[1]
        s_left = h @ a_sa[0, :Hd]
        s_right = h @ a_sa[0, Hd:]
        scores = s_left[:, None] + s_right[None, :]
        e = jnp.where(adj_a != 0, jnp.exp(-jax.nn.leaky_relu(scores, 0.01)), 0.0)
        attn = e / (jnp.sum(e, axis=1, keepdims=True) + 1e-05)
        x_a = attn @ h
        x_b = adj_b @ (x @ W_gcnb) + b_gcnb
        return jax.nn.sigmoid(attn_a * x_a + attn_b * x_b)

    def _L2_gnn_ref(input_features, adj, W, b):
        import jax, jax.numpy as jnp
        import numpy as np
        N = 4096
        F_IN = 256
        F_OUT = 256
        DENSITY = 0.01
        A = (adj != 0).astype(input_features.dtype)
        hidden = input_features @ W + b
        deg = jnp.sum(A, axis=0)
        return A @ hidden / deg[:, None]

    def _L3_gnn_ref(inputs, adj, W_stack):
        import jax, jax.numpy as jnp
        import numpy as np
        N = 4096
        D = 256
        L = 2
        NEG_SLOPE = 0.01

        def _gat_layer(x, W, adj):
            proj = x @ W
            Wh, Ws = jnp.split(proj, 2, axis=-1)
            scores = Wh @ Ws.T
            a = jax.nn.softmax(scores, axis=-1) * adj
            out = a @ Wh
            out = out + x
            return jax.nn.leaky_relu(out, NEG_SLOPE)
        x = inputs
        for l in range(W_stack.shape[0]):
            x = _gat_layer(x, W_stack[l], adj)
        return x
    x = _layernorm(x + _L0_gnn_ref(x, adj, L0_gnn_weight), axis=-1)
    x = _layernorm(x + _L1_gnn_ref(x, adj, adj, L1_gnn_W_sa, L1_gnn_a_sa, L1_gnn_W_gcnb, L1_gnn_b_gcnb, L1_gnn_Wa, L1_gnn_ba, L1_gnn_Wb, L1_gnn_bb), axis=-1)
    x = _layernorm(x + _L2_gnn_ref(x, adj, L2_gnn_W, L2_gnn_b), axis=-1)
    x = _layernorm(x + _L3_gnn_ref(x, adj, L3_gnn_W_stack), axis=-1)
    return x

_drawn_inputs = setup_inputs


def setup_inputs(seed=0):
    import zlib

    import numpy as np

    out = dict(_drawn_inputs(seed))
    spreads = {}
    factors = {'L1_gnn_a_sa': 8.0, 'L1_gnn_b_gcnb': 8.0, 'L2_gnn_b': 8.0, 'L3_gnn_W_stack': 2.689}
    for name, (base, spread) in spreads.items():
        noise = np.random.default_rng([zlib.crc32(name.encode()), seed]).standard_normal(out[name].shape)
        drawn = base * np.exp(spread * noise) if base else spread * noise
        out[name] = jnp.asarray(drawn.astype(out[name].dtype))
    for name, factor in factors.items():
        out[name] = (out[name] * factor).astype(out[name].dtype)
    return out
```

```python
from contextlib import ExitStack

import concourse.bass as bass
from concourse import mybir

F32 = mybir.dt.float32
F32R = mybir.dt.float32r
BF16 = mybir.dt.bfloat16
ALU = mybir.AluOpType
ACT = mybir.ActivationFunctionType
AX = mybir.AxisListType

P = 128
BANK = 512
LN_EPS = 1e-5
ATTN_EPS = 1e-5
SLOPE = 0.01
MASKED = -3.0e38


class Count:

    def __init__(self, sem, credit=0):
        self.sem, self.credit = sem, credit

    def done(self, n):
        return n + self.credit

    def room(self, i):
        return i + 1


class Chain:

    def __init__(self, eng, sem, steps, i):
        self.eng, self.sem, self.base, self.steps, self.n = eng, sem, i * steps, steps, 0

    def link(self, ins):
        self.n += 1
        assert self.n <= self.steps
        ins.then_inc(self.sem, 1)
        self.eng.wait_ge(self.sem, self.base + self.n)


def pipeline(eng, tiles, stages, apart=0):
    end = tiles - apart
    deep = max(lag for _, lag in stages)

    def step(s, parity, lo, hi):
        for stage, lag in stages:
            if lo - lag >= 0 and hi - lag < tiles:
                stage(s - lag, (parity - lag) % 2)

    first = deep + (end - deep) % 2
    for s in range(first):
        step(s, s % 2, s, s)
    with eng.Fori(0, (end - first) // 2) as turn:
        for d in range(2):
            step(turn * 2 + (first + d), (first + d) % 2, first, end - 1)
    for s in range(end, tiles + deep):
        step(s, s % 2, s, s)


def gnn_stack(nc, x, adj, w0, w_sa, a_sa, w_gcn, b_gcn, wa, ba, wb, bb, w2, b2, w3, out):
    N, D = x.shape
    T = -(-N // P)
    FULL = N // P
    TAIL = N - FULL * P
    NP = T * P
    KD = D // P
    assert D == 2 * P and T - FULL == 1 and w3.shape[0] == 2
    CH = [(c, min(c + BANK, N)) for c in range(0, N, BANK)]
    EB = BANK // P

    def kk(k):
        return P if k < FULL else TAIL

    ctx = ExitStack()
    with ctx:
        ctx.enter_context(nc.allow_non_contiguous_dma(reason="weight vectors as columns"))

        def sb(name, shape, dt=F32):
            return ctx.enter_context(nc.sbuf_tensor(name, shape, dt))

        def sem(name, credit=0):
            s = Count(ctx.enter_context(nc.semaphore(name)), credit)
            counts.append(s)
            return s

        counts = []

        adjT = sb("adjT", [P, T, NP])
        x_all = sb("x_all", [P, T, D])
        feats = sb("feats", [P, T, 2, D + 2])
        xs = sb("xs", [P, 2, D])
        xTs = sb("xTs", [P, 2, KD, P])
        vbuf = sb("vbuf", [P, 2, D])
        proj_s = sb("proj_s", [P, 2, 2 * D])
        WhTs = sb("WhTs", [P, 2, KD, P])
        ident = sb("ident", [P, P])
        identb = sb("identb", [P, P], BF16)
        W1 = sb("W1", [P, KD, 2 * D])
        Wcol = sb("Wcol", [P, KD, 6])
        nwl = sb("nwl", [P, KD])
        WLb = sb("WLb", [P, KD, P])
        W2 = sb("W2", [P, KD, D])
        W3 = sb("W3", [P, 2, KD, 2 * D])
        b1b = sb("b1b", [P, D])
        b2b = sb("b2b", [P, D])
        babb = sb("babb", [P, 2])
        hbab = sb("hbab", [P, 2])
        hattn = sb("hattn", [P, T, 2])
        nsr = sb("nsr", [P, T, 1])
        nsl = sb("nsl", [P, NP])
        deg = sb("deg", [P, T])
        rdeg = sb("rdeg", [P, T])
        padone = sb("padone", [P, 1])
        nhalf = sb("nhalf", [P, 1])
        stats = sb("stats", [P, 2, 6])
        mv = sb("mv", [P, 2, 2])
        veps = sb("veps", [P, 2, 1])
        rstd = sb("rstd", [P, 2, 1])
        att_in = sb("att_in", [P, 2, 2])
        att_t = sb("att_t", [P, 2, 2])
        att = sb("att", [P, 2, 2])
        den = sb("den", [P, 2, 1])
        rden = sb("rden", [P, 2, 1])
        idle = sb("idle", [P, 1])
        negmax = sb("negmax", [P, 2, 1])
        esum = sb("esum", [P, 2, 1])

        SLOT = T * D * 4
        arena = sb("arena", [P, 7 * T * D])
        base = nc.sbuf_base - 7 * SLOT

        def at(name, slot, shape, dt=F32, skip=0):
            return nc.alloc_sbuf_tensor_at(name, shape, dt, offset=base + slot * SLOT + skip)

        adj_rows = at("adj_rows", 0, [P, 2, NP])
        xw = at("xw", 1, [P, T, D], F32R)
        hi = at("hi", 2, [P, 2, T, P], F32R)
        lo = at("lo", 3, [P, 2, T, P], F32R)
        adjTs = at("adjTs", 0, [P, 2, T, P])
        escore = at("escore", 1, [P, 2, T, P])
        eT = at("eT", 3, [P, 2, T, P])
        hid = at("hid", 4, [P, T, 2 * D], F32R)
        maskT = at("maskT", 2, [P, 2, T, P], F32R)
        probs = at("probs", 2, [P, 2, NP])
        probsT = at("probsT", 3, [P, 2, T, P])
        WT = [at("WT0", 0, [P, 2 * KD, NP]), at("WT1", 4, [P, 2 * KD, NP])]
        x1 = at("x1", 6, [P, T, D])
        w0n = at("w0n", 4, [P, KD, D])
        w0neg = at("w0neg", 5, [P, KD, D], BF16)
        KB = 2 * KD * D
        w0s = at("w0s", 6, [P, KD, D], BF16)
        w0T = at("w0T", 6, [P, KD, D], BF16, KB)
        pos = at("pos", 6, [P, 2, D], BF16, 2 * KB)
        posT = at("posT", 6, [P, 2, KD, P], BF16, 3 * KB)
        a_b = at("a_b", 6, [P, 2 * D], F32, 4 * KB)
        junk = sb("junk", [P, D])

        psum = ctx.enter_context(nc.psum_tensor("psum", [P, 8, BANK], F32))
        Wh = [feats[:, :, 0, 0:D], feats[:, :, 1, 0:D]]

        def bank(b, lo_=0, hi_=BANK):
            return psum[:, b, lo_:hi_]

        def bankb(b):
            return psum[:, b, :].bitcast(BF16)

        adj_in_tail = sem("adj_in_tail")
        adj_in = [sem("adj_in_even"), sem("adj_in_odd")]
        x_in, w0_in, w_in, a_in, col_in = sem("x_in"), sem("w0_in"), sem("w_in"), sem("a_in"), sem("col_in")
        pads_zero = sem("pads_zero")
        out_done = [sem("out_done_even", 16), sem("out_done_odd", 16)]
        dve_setup, consts_ready = sem("dve_setup"), sem("consts_ready")
        ident_ready, w0_signed, w0T_ps, w0T_ready = sem("ident_ready"), sem("w0_signed"), sem("w0T_ps"), sem("w0T_ready")
        cols_ready = sem("cols_ready")
        pos_ready, pos_ps, posT_ready, xw_ps, xw_ready = (
            sem("pos_ready"), sem("pos_ps", 2), sem("posT_ready", 2), sem("xw_ps", 2), sem("xw_ready", 2))

        class Phase:

            def __init__(s, n):
                s.agg_done = sem(n + "_agg_done", 2)
                s.acc_read = sem(n + "_acc_read", 2)
                s.fin_chain = sem(n + "_fin_chain")
                s.var_ready = sem(n + "_var_ready")
                s.rstd_ready = sem(n + "_rstd_ready")
                s.xs_ready = sem(n + "_xs_ready")
                s.x_stored = sem(n + "_x_stored", 2)
                s.xs_turned = sem(n + "_xs_turned", 2)
                s.xT_ready = sem(n + "_xT_ready", 1)
                s.proj_done = sem(n + "_proj_done", 2)
                s.proj_ready = sem(n + "_proj_ready", 1)

        A, B, C, D1, D2 = (Phase(n) for n in ("binary", "attn", "mean", "gat1", "gat2"))
        BANKS_T = -(-T // EB)
        adjT_turned = sem("adjT_turned", 2 * BANKS_T)
        adjT_banks_read = sem("adjT_banks_read", BANKS_T)
        hi_ready, lo_ready = sem("hi_ready"), sem("lo_ready")
        bprep_adj, bprep_mask, bprep_score, bprep_exp = (
            sem("stationary_adj_ready"), sem("mask_ready"), sem("score_ready"), sem("exp_ready"))
        aggz_done, score_chain, pool_chain = sem("aggz_done", 2), sem("score_chain"), sem("pool_chain")
        att_in_ready, att_ready, gate_in_ready, gate_ready = (
            sem("att_in_ready"), sem("att_ready"), sem("gate_in_ready"), sem("gate_ready"))
        deg_ready = sem("deg_ready")
        hid_chain = sem("hid_chain")
        mask_ready = sem("mean_mask_ready")

        class Gat:
            def __init__(s, n):
                s.WhTs_ready = sem(n + "_WhTs_ready")
                s.scores_done = sem(n + "_scores_done", 2)
                s.max_ready = sem(n + "_max_ready", 1)
                s.probs_ready = sem(n + "_probs_ready", 1)
                s.turned = sem(n + "_turned", 2)
                s.probsT_ready = sem(n + "_probsT_ready", 1)

        G = [Gat("g1"), Gat("g2")]

        class Turn:

            def __init__(s, n):
                s.proj_s_ready = sem(n + "_proj_s_ready", 1)
                s.turned = sem(n + "_WT_turned", 2)
                s.WT_ready = sem(n + "_WT_ready", 1)

        TC, TD = Turn("mean"), Turn("gat1")

        block = ctx.enter_context(nc.Block())

        def credits(eng, *cs):
            for c in cs:
                eng.sem_inc(c.sem, c.credit)

        @block.sync
        def _(sp):
            sp.dma_start(x_all[:, 0:FULL, :], x[0:FULL * P, :].rearrange("(t p) d -> p t d", p=P)).then_inc(x_in.sem, 16)
            sp.dma_start(w0n[:, :, :], w0.rearrange("(k p) d -> p k d", p=P)).then_inc(w0_in.sem, 16)

            def load_rows(i, p):
                sp.wait_ge(adjT_turned.sem, (i + 1) * BANKS_T)
                sp.dma_start(adj_rows[:, p, 0:N], adj[i * P:(i + 1) * P, :] if isinstance(i, int) else
                             adj[bass.ds(i * P, P), :]).then_inc(adj_in[p].sem, 16)

            sp.wait_ge(pads_zero.sem, 1)
            with sp.Fori(0, FULL // 2) as pair:
                load_rows(pair * 2, 0)
                load_rows(pair * 2 + 1, 1)
            sp.wait_ge(adjT_turned.sem, (FULL + 1) * BANKS_T)
            sp.dma_start(adj_rows[0:64, 0, 0:N], adj[FULL * P:FULL * P + 64, :]).then_inc(adj_in_tail.sem, 16)
            sp.dma_start(adj_rows[64:TAIL, 0, 0:N], adj[FULL * P + 64:N, :]).then_inc(adj_in_tail.sem, 16)

            def store(i, p):
                sp.wait_ge(D2.xs_ready.sem, D2.xs_ready.done(i + 1))
                sp.dma_start(out[bass.ds(i * P, P), :], xs[:, p, :]).then_inc(out_done[p].sem, 16)

            with sp.Fori(0, FULL // 2) as pair:
                store(pair * 2, 0)
                store(pair * 2 + 1, 1)
            sp.wait_ge(D2.xs_ready.sem, D2.xs_ready.done(T))
            sp.dma_start(out[FULL * P:N, :], xs[0:TAIL, 0, :]).then_inc(out_done[0].sem, 16)
            sp.wait_ge(out_done[0].sem, 16 * (T + 1) // 2 + out_done[0].credit)
            sp.wait_ge(out_done[1].sem, 16 * (T // 2) + out_done[1].credit)

        @block.gpsimd
        def _(pool):
            credits(pool, A.x_stored, B.x_stored, C.x_stored, D1.x_stored)
            nc.gpsimd.memset(ident[:, :], 0.0).then_inc(pool_chain.sem, 1)
            nc.gpsimd.memset(identb[:, :], 0.0).then_inc(pool_chain.sem, 1)
            nc.gpsimd.memset(nhalf[:, :], -0.5).then_inc(consts_ready.sem, 1)
            pool.wait_ge(pool_chain.sem, 2)
            for m in (ident, identb):
                nc.gpsimd.affine_select(out=m[:, :], in_=m[:, :], compare_op=ALU.not_equal, fill=1.0, base=0,
                                        pattern=[[-1, P]], channel_multiplier=1).then_inc(ident_ready.sem, 1)
            pool.wait_ge(consts_ready.sem, 1)

            def rsqrt(ph):
                def stage(i, p):
                    pool.wait_ge(ph.var_ready.sem, ph.var_ready.done(i + 1))
                    nc.gpsimd.tensor_tensor(rstd[:, p, :], veps[:, p, :], nhalf[:, :], ALU.pow).then_inc(ph.rstd_ready.sem, 1)
                return stage

            def store_x(ph, dst):
                def stage(i, p):
                    pool.wait_ge(ph.xs_ready.sem, ph.xs_ready.done(i + 1))
                    nc.gpsimd.tensor_copy(dst[:, bass.ds(i, 1), :], xs[:, p:p + 1, :]).then_inc(ph.x_stored.sem, 1)
                return stage

            pipeline(pool, T, [(rsqrt(A), 1), (store_x(A, x_all), 1)])

            def prep(i, p):
                if isinstance(i, int) and i == 0:
                    pool.wait_ge(A.agg_done.sem, A.agg_done.done(T))
                pool.wait_ge(aggz_done.sem, aggz_done.room(i))
                nc.gpsimd.tensor_copy(adjTs[:, p, :, :], adjT[:, :, bass.ds(i * P, P)]).then_inc(bprep_adj.sem, 1)
                pool.wait_ge(ident_ready.sem, 2)
                pool.wait_ge(bprep_adj.sem, i + 1)
                pool.wait_ge(B.agg_done.sem, B.agg_done.room(i))
                nc.gpsimd.tensor_scalar(escore[:, p, :, :], adjTs[:, p, :, :], 0.0, MASKED, ALU.is_equal,
                                        ALU.mult).then_inc(bprep_mask.sem, 1)

            pipeline(pool, T, [(prep, 0), (rsqrt(B), 1), (store_x(B, x_all), 1)])
            pipeline(pool, T, [(rsqrt(C), 1), (store_x(C, x_all), 1)])

            def stage_WhT(g, t, wt, done):
                def stage(i, p):
                    if isinstance(i, int) and i == 0:
                        pool.wait_ge(t.WT_ready.sem, t.WT_ready.done(T))
                    pool.wait_ge(g.scores_done.sem, g.scores_done.room(i))
                    nc.gpsimd.tensor_copy(WhTs[:, p, :, :], wt[:, 0:KD, bass.ds(i * P, P)]).then_inc(g.WhTs_ready.sem, 1)
                return stage

            pipeline(pool, T, [(stage_WhT(G[0], TC, WT[0], None), 0), (store_x(D1, x1), 2)])
            pipeline(pool, T, [(stage_WhT(G[1], TD, WT[1], None), 0), (rsqrt(D2), 2)])

        @block.scalar
        def _(act):
            credits(act, posT_ready, A.xT_ready, B.xT_ready, C.xT_ready, D1.xT_ready, adjT_banks_read,
                    TC.proj_s_ready, TD.proj_s_ready, TC.WT_ready, TD.WT_ready, G[0].probs_ready, G[1].probs_ready)
            act.wait_ge(pads_zero.sem, 1)
            act.dma_start(x_all[0:64, FULL, :], x[FULL * P:FULL * P + 64, :]).then_inc(x_in.sem, 16)
            act.dma_start(x_all[64:TAIL, FULL, :], x[FULL * P + 64:N, :]).then_inc(x_in.sem, 16)
            act.dma_start(a_b[:, :], a_sa.partition_broadcast(P).rearrange("p a d -> p (a d)")).then_inc(a_in.sem, 16)
            act.dma_start(W1[:, :, 0:D], w_gcn.rearrange("(k p) n -> p k n", p=P)).then_inc(w_in.sem, 16)
            act.dma_start(W1[:, :, D:2 * D], w_sa.rearrange("(k p) n -> p k n", p=P)).then_inc(w_in.sem, 16)
            for n, w in enumerate((wa, wb)):
                for half in range(2):
                    for k in range(KD):
                        c = (half * KD + k) * P
                        act.dma_start(Wcol[:, k, 2 * half + n:2 * half + n + 1],
                                      w[:, c:c + P].rearrange("a p -> p a")).then_inc(col_in.sem, 16)
            act.dma_start(b1b[:, :], b_gcn.partition_broadcast(P)).then_inc(w_in.sem, 16)
            act.dma_start(b2b[:, :], b2.partition_broadcast(P)).then_inc(w_in.sem, 16)
            act.dma_start(babb[:, 0:1], ba.partition_broadcast(P)).then_inc(w_in.sem, 16)
            act.dma_start(babb[:, 1:2], bb.partition_broadcast(P)).then_inc(w_in.sem, 16)
            act.dma_start(W2[:, :, :], w2.rearrange("(k p) n -> p k n", p=P)).then_inc(w_in.sem, 16)
            for l in range(2):
                act.dma_start(W3[:, l, :, :], w3[l].rearrange("(k p) n -> p k n", p=P)).then_inc(w_in.sem, 16)

            act.wait_ge(w0T_ps.sem, 1)
            nc.scalar.activation(w0T[:, :, :], bankb(7)[:, 0:KD * D].rearrange("p (k n) -> p k n", k=KD),
                                 ACT.Copy).then_inc(w0T_ready.sem, 1)

            def pos_evac(i, p):
                act.wait_ge(pos_ps.sem, pos_ps.done(i + 1))
                act.wait_ge(xw_ps.sem, xw_ps.room(i))
                nc.scalar.activation(posT[:, p, :, :], bankb(5 + p)[:, 0:D].rearrange("p (k n) -> p k n", k=KD),
                                     ACT.Copy).then_inc(posT_ready.sem, 1)

            pipeline(act, T, [(pos_evac, 0)])

            def xT_evac(ph, b):
                def stage(i, p):
                    act.wait_ge(ph.xs_turned.sem, ph.xs_turned.done(i + 1))
                    act.wait_ge(ph.proj_done.sem, ph.proj_done.room(i))
                    nc.scalar.activation(xTs[:, p, :, :], bank(b, 0, D).rearrange("p (k n) -> p k n", k=KD),
                                         ACT.Copy).then_inc(ph.xT_ready.sem, 1)
                return stage

            def adj_evac(i, p):
                act.wait_ge(A.agg_done.sem, A.agg_done.room(i))
                for g in range(BANKS_T):
                    k0, k1 = g * EB, min(g * EB + EB, T)
                    act.wait_ge(adjT_turned.sem, adjT_turned.done(i * BANKS_T + g + 1))
                    src = bank(g, 0, (k1 - k0) * P).rearrange("p (k n) -> p k n", n=P)
                    nc.scalar.activation(adjT[:, k0:k1, bass.ds(i * P, P)], src, ACT.Copy)
                    last = nc.scalar.activation(hi[:, p, k0:k1, :], src, ACT.Copy)
                    last.then_inc(adjT_banks_read.sem, 1)

            pipeline(act, T, [(xT_evac(A, 5), 3), (adj_evac, 0)])

            def exp_scores(i, p):
                act.wait_ge(bprep_score.sem, i + 1)
                act.wait_ge(B.agg_done.sem, B.agg_done.room(i))
                nc.scalar.activation(eT[:, p, :, :], escore[:, p, :, :], ACT.Exp).then_inc(bprep_exp.sem, 1)

            def gates(i, p):
                act.wait_ge(att_in_ready.sem, i + 1)
                nc.scalar.activation(att_t[:, p, :], att_in[:, p, :], ACT.Tanh).then_inc(att_ready.sem, 1)
                act.wait_ge(gate_in_ready.sem, i + 1)
                nc.scalar.activation(vbuf[:, p, :], vbuf[:, p, :], ACT.Tanh, scale=0.5).then_inc(gate_ready.sem, 1)

            pipeline(act, T, [(xT_evac(B, 5), 3), (exp_scores, 0), (gates, 1)])

            def proj_evac(ph, t, wh):
                def stage(i, p):
                    act.wait_ge(ph.proj_done.sem, ph.proj_done.done(i + 1))
                    act.wait_ge(t.turned.sem, t.turned.room(i))
                    nc.scalar.activation(wh[:, bass.ds(i, 1), :], bank(7, 0, D).unsqueeze(1), ACT.Copy)
                    nc.scalar.activation(proj_s[:, p, :], bank(7), ACT.Copy).then_inc(t.proj_s_ready.sem, 1)
                return stage

            def WT_evac(t, wt, b):
                def stage(i, p):
                    act.wait_ge(t.turned.sem, t.turned.done(i + 1))
                    nc.scalar.activation(wt[:, :, bass.ds(i * P, P)], bank(b).rearrange("p (m n) -> p m n", n=P),
                                         ACT.Copy).then_inc(t.WT_ready.sem, 1)
                return stage

            pipeline(act, T, [(WT_evac(TC, WT[0], 6), 4), (xT_evac(C, 5), 3), (proj_evac(C, TC, Wh[0]), 3)])

            def exp_row(g):
                def stage(i, p):
                    act.wait_ge(g.max_ready.sem, g.max_ready.done(i + 1))
                    act.wait_ge(g.turned.sem, g.turned.room(i))
                    nc.scalar.activation(probs[:, p, 0:N], psum[:, 0:len(CH), :].rearrange("p b n -> p (b n)")[:, 0:N],
                                         ACT.Exp, bias=negmax[:, p, :], accum_out=esum[:, p, :]).then_inc(g.probs_ready.sem, 1)
                return stage

            pipeline(act, T, [(xT_evac(D1, 7), 3), (exp_row(G[0]), 0), (proj_evac(D1, TD, Wh[1]), 3), (WT_evac(TD, WT[1], 7), 3)])
            pipeline(act, T, [(exp_row(G[1]), 0)])

        @block.vector
        def _(dve):
            credits(dve, xw_ready, A.acc_read, B.acc_read, C.acc_read, D1.acc_read, D2.acc_read,
                    A.proj_ready, B.proj_ready, G[0].max_ready, G[1].max_ready, G[0].probsT_ready, G[1].probsT_ready)
            for o in out_done:
                dve.sem_inc(o.sem, o.credit)
            nc.vector.memset(x_all[:, FULL, :], 0.0)
            nc.vector.memset(adj_rows[:, :, N:NP], 0.0).then_inc(pads_zero.sem, 1)
            nc.vector.memset(feats[:, :, 1, D:D + 2], 1.0)
            nc.vector.memset(WLb[:, :, :], 0.0).then_inc(dve_setup.sem, 1)
            nc.vector.memset(padone[:, :], 1.0).then_inc(dve_setup.sem, 1)
            dve.wait_ge(dve_setup.sem, 2)
            nc.vector.memset(padone[0:TAIL, :], 0.0)
            dve.wait_ge(w0_in.sem, 16)
            nc.vector.tensor_scalar(w0neg[:, :, :], w0n[:, :, :], 0.0, None, ALU.is_lt).then_inc(dve_setup.sem, 1)
            dve.wait_ge(dve_setup.sem, 3)
            nc.vector.scalar_tensor_tensor(out=w0s[:, :, :], in0=w0n[:, :, :], scalar=0.0, in1=w0neg[:, :, :],
                                           op0=ALU.is_gt, op1=ALU.subtract).then_inc(w0_signed.sem, 1)
            dve.wait_ge(x_in.sem, 48)

            def positive(i, p):
                dve.wait_ge(pos_ps.sem, pos_ps.room(i))
                nc.vector.tensor_scalar(pos[:, p:p + 1, :], x_all[:, bass.ds(i, 1), :], 0.0, None,
                                        ALU.is_gt).then_inc(pos_ready.sem, 1)

            def xw_evac(i, p):
                dve.wait_ge(xw_ps.sem, xw_ps.done(i + 1))
                nc.vector.tensor_copy(xw[:, bass.ds(i, 1), :], bank(3 + p, 0, D).unsqueeze(1)).then_inc(xw_ready.sem, 1)

            pipeline(dve, T, [(positive, 0), (xw_evac, 1)])

            dve.wait_ge(a_in.sem, 16)
            dve.wait_ge(w_in.sem, 16 * 9)
            dve.wait_ge(col_in.sem, 16 * 8)
            for half, dst in ((0, nwl), (1, None)):
                for k in range(KD):
                    acc = nwl[:, k:k + 1] if half == 0 else Wcol[:, k, 4:5]
                    nc.vector.tensor_tensor_reduce(out=junk[:, :], in0=W1[:, k, D:2 * D],
                                                   in1=a_b[:, half * D:(half + 1) * D], scale=-1.0, scalar=0.0,
                                                   op0=ALU.mult, op1=ALU.add, accum_out=acc).then_inc(dve_setup.sem, 1)
                    dve.wait_ge(dve_setup.sem, 4 + half * KD + k)
            for k in range(KD):
                nc.vector.tensor_scalar(WLb[:, k, :], WLb[:, k, :], nwl[:, k:k + 1], None, ALU.add)
            nc.vector.tensor_scalar(hbab[:, :], babb[:, :], 0.5, None, ALU.mult).then_inc(cols_ready.sem, 1)
            dve.wait_ge(cols_ready.sem, 1)

            def norm(ph, i, p, c, free):
                c.link(nc.vector.bn_stats(stats[:, p, :], vbuf[:, p, :]))
                nc.vector.memset(idle[:, :], 0.0)
                c.link(nc.vector.bn_aggr(mv[:, p, :], stats[:, p, :]))
                nc.vector.tensor_scalar(veps[:, p, :], mv[:, p, 1:2], LN_EPS, None, ALU.add).then_inc(ph.var_ready.sem, 1)
                free(i, p)
                dve.wait_ge(ph.rstd_ready.sem, i + 1)
                nc.vector.tensor_scalar(xs[:, p, :], vbuf[:, p, :], mv[:, p, 0:1], rstd[:, p, :], ALU.subtract,
                                        ALU.mult).then_inc(ph.xs_ready.sem, 1)

            def xs_free(ph):
                def free(i, p):
                    dve.wait_ge(ph.xs_turned.sem, ph.xs_turned.room(i))
                    dve.wait_ge(ph.x_stored.sem, ph.x_stored.room(i))
                return free

            def lower_bits(i, p):
                dve.wait_ge(adjT_banks_read.sem, adjT_banks_read.done(BANKS_T * (i + 1)))
                dve.wait_ge(A.agg_done.sem, A.agg_done.room(i))
                nc.vector.tensor_tensor(lo[:, p, :, :], adjT[:, :, bass.ds(i * P, P)], hi[:, p, :, :].bitcast(F32),
                                        ALU.subtract).then_inc(lo_ready.sem, 1)

            def finish_a(i, p):
                c = Chain(dve, A.fin_chain.sem, 3, i)
                dve.wait_ge(A.agg_done.sem, A.agg_done.done(i + 1))
                ins = nc.vector.scalar_tensor_tensor(out=vbuf[:, p:p + 1, :], in0=bank(3 + p, 0, D).unsqueeze(1), scalar=0.0,
                                                     in1=x_all[:, bass.ds(i, 1), :], op0=ALU.max, op1=ALU.add)
                c.link(ins)
                norm(A, i, p, c, xs_free(A))

            def evac_a(i, p):
                dve.wait_ge(A.proj_done.sem, A.proj_done.done(i + 1))
                nc.vector.tensor_copy(feats[:, bass.ds(i, 1), :, 0:D],
                                      bank(7).rearrange("p (a b n) -> p a b n", a=1, b=2))
                nc.vector.tensor_copy(feats[:, bass.ds(i, 1), 0:1, D:D + 2], bank(6, 0, 2).unsqueeze(1).unsqueeze(1))
                nc.vector.scalar_tensor_tensor(out=hattn[:, bass.ds(i, 1), :], in0=bank(6, 2, 4).unsqueeze(1), scalar=0.5,
                                               in1=hbab[:, :].unsqueeze(1), op0=ALU.mult, op1=ALU.add)
                nc.vector.tensor_copy(nsr[:, bass.ds(i, 1), :], bank(6, 4, 5).unsqueeze(1))
                nc.vector.tensor_copy(nsl[:, bass.ds(i * P, P)], bank(6, P, 2 * P)).then_inc(A.proj_ready.sem, 1)

            pipeline(dve, T, [(lower_bits, 0), (evac_a, 3), (finish_a, 1)])

            def scores_b(i, p):
                c = Chain(dve, score_chain.sem, 1, i)
                if isinstance(i, int) and i == 0:
                    dve.wait_ge(A.proj_ready.sem, A.proj_ready.done(T))
                dve.wait_ge(bprep_mask.sem, i + 1)
                for k in range(T):
                    ins = nc.vector.scalar_tensor_tensor(out=escore[:, p, k, :], in0=escore[:, p, k, :], scalar=nsr[:, k, :],
                                                         in1=nsl[:, bass.ds(i * P, P)], op0=ALU.add, op1=ALU.add)
                c.link(ins)
                nc.vector.scalar_tensor_tensor(out=escore[:, p, :, :], in0=escore[:, p, :, :], scalar=SLOPE,
                                               in1=escore[:, p, :, :], op0=ALU.mult, op1=ALU.min).then_inc(bprep_score.sem, 1)

            def finish_b(i, p):
                c = Chain(dve, B.fin_chain.sem, 10, i)
                dve.wait_ge(aggz_done.sem, aggz_done.done(i + 1))
                nc.vector.scalar_tensor_tensor(out=att_in[:, p:p + 1, :], in0=bank(p, D, D + 2).unsqueeze(1), scalar=0.5,
                                               in1=hattn[:, bass.ds(i, 1), :], op0=ALU.mult, op1=ALU.add).then_inc(att_in_ready.sem, 1)
                c.link(nc.vector.tensor_tensor(vbuf[:, p, :], bank(p, 0, D), b1b[:, :], ALU.add))
                dve.wait_ge(att_ready.sem, i + 1)
                c.link(nc.vector.tensor_scalar(att[:, p, :], att_t[:, p, :], 0.5, 0.5, ALU.mult, ALU.add))
                c.link(nc.vector.tensor_scalar(vbuf[:, p, :], vbuf[:, p, :], att[:, p, 1:2], None, ALU.mult))
                dve.wait_ge(B.agg_done.sem, B.agg_done.done(i + 1))
                c.link(nc.vector.tensor_scalar(den[:, p, :], bank(2 + p, D, D + 1), ATTN_EPS, None, ALU.add))
                c.link(nc.vector.reciprocal(rden[:, p, :], den[:, p, :]))
                c.link(nc.vector.tensor_tensor(rden[:, p, :], rden[:, p, :], att[:, p, 0:1], ALU.mult))
                nc.vector.scalar_tensor_tensor(out=vbuf[:, p, :], in0=bank(2 + p, 0, D), scalar=rden[:, p, :], in1=vbuf[:, p, :],
                                               op0=ALU.mult, op1=ALU.add).then_inc(gate_in_ready.sem, 1)
                dve.wait_ge(gate_ready.sem, i + 1)
                c.link(nc.vector.tensor_scalar(vbuf[:, p, :], vbuf[:, p, :], 0.5, 0.5, ALU.mult, ALU.add))
                c.link(nc.vector.tensor_tensor(vbuf[:, p:p + 1, :], vbuf[:, p:p + 1, :], x_all[:, bass.ds(i, 1), :], ALU.add))
                norm(B, i, p, c, xs_free(B))

            def evac_b(i, p):
                c = Chain(dve, hid_chain.sem, 2, i)
                dve.wait_ge(B.proj_done.sem, B.proj_done.done(i + 1))
                ins = nc.vector.tensor_tensor(junk[:, :], bank(7, 0, D), b2b[:, :], ALU.add)
                ins.then_inc(B.proj_ready.sem, 1)
                dve.wait_ge(B.proj_ready.sem, B.proj_ready.done(i + 1))
                c.link(nc.vector.tensor_copy(hid[:, bass.ds(i, 1), 0:D], junk[:, :].unsqueeze(1)))
                c.link(nc.vector.tensor_tensor(hid[:, bass.ds(i, 1), D:2 * D], junk[:, :].unsqueeze(1),
                                               hid[:, bass.ds(i, 1), 0:D].bitcast(F32), ALU.subtract))

            pipeline(dve, T, [(scores_b, 0), (evac_b, 3), (finish_b, 1)])

            for k in range(T):
                nc.vector.tensor_scalar(probs[:, 0, 0:N], adjT[:, k, 0:N], 0.0, 0.0, ALU.not_equal, ALU.add,
                                        accum_out=deg[:, k:k + 1]).then_inc(deg_ready.sem, 1)
                dve.wait_ge(deg_ready.sem, k + 1)
            nc.vector.tensor_tensor(deg[:, FULL:T], deg[:, FULL:T], padone[:, :], ALU.add).then_inc(deg_ready.sem, 1)
            dve.wait_ge(deg_ready.sem, T + 1)
            nc.vector.reciprocal(rdeg[:, :], deg[:, :]).then_inc(deg_ready.sem, 1)
            dve.wait_ge(deg_ready.sem, T + 2)

            def mask(i, p):
                dve.wait_ge(C.agg_done.sem, C.agg_done.room(i))
                nc.vector.tensor_scalar(maskT[:, p, :, :], adjT[:, :, bass.ds(i * P, P)], 0.0, None,
                                        ALU.not_equal).then_inc(mask_ready.sem, 1)

            def finish_c(i, p):
                c = Chain(dve, C.fin_chain.sem, 4, i)
                dve.wait_ge(C.agg_done.sem, C.agg_done.done(i + 1))
                r = rdeg[:, bass.ds(i, 1)]
                c.link(nc.vector.scalar_tensor_tensor(out=vbuf[:, p:p + 1, :], in0=bank(3 + p, 0, D).unsqueeze(1), scalar=r,
                                                      in1=x_all[:, bass.ds(i, 1), :], op0=ALU.mult, op1=ALU.add))
                c.link(nc.vector.scalar_tensor_tensor(out=vbuf[:, p, :], in0=bank(3 + p, D, 2 * D), scalar=r, in1=vbuf[:, p, :],
                                                      op0=ALU.mult, op1=ALU.add))
                norm(C, i, p, c, xs_free(C))

            pipeline(dve, T, [(mask, 0), (finish_c, 1)])

            nc.vector.memset(probs[:, :, N:NP], 0.0).then_inc(pads_zero.sem, 1)

            def turn_evac(g):
                def stage(i, p):
                    dve.wait_ge(g.turned.sem, g.turned.done(i + 1))
                    nc.vector.tensor_tensor(probsT[:, p, :, :], psum[:, 3:3 + BANKS_T, :].rearrange("p b (k n) -> p (b k) n", n=P)[:, 0:T, :],
                                            adjT[:, :, bass.ds(i * P, P)], ALU.mult).then_inc(g.probsT_ready.sem, 1)
                return stage

            def row_max(g):
                def stage(i, p):
                    dve.wait_ge(g.scores_done.sem, g.scores_done.done(i + 1))
                    nc.vector.tensor_reduce(negmax[:, p, :], psum[:, 0:len(CH), :].rearrange("p b n -> p (b n)")[:, 0:N], AX.X,
                                            ALU.max, negate=True).then_inc(g.max_ready.sem, 1)
                return stage

            def gat_out(ph, c, i, p, xin):
                dve.wait_ge(ph.agg_done.sem, ph.agg_done.done(i + 1))
                c.link(nc.vector.reciprocal(rden[:, p, :], esum[:, p, :]))
                ins = nc.vector.scalar_tensor_tensor(out=vbuf[:, p:p + 1, :], in0=bank(6, 0, D).unsqueeze(1), scalar=rden[:, p, :],
                                                     in1=xin[:, bass.ds(i, 1), :], op0=ALU.mult, op1=ALU.add)
                ins.then_inc(ph.acc_read.sem, 1)
                dve.wait_ge(ph.acc_read.sem, ph.acc_read.done(i + 1))

            def finish_d1(i, p):
                c = Chain(dve, D1.fin_chain.sem, 1, i)
                gat_out(D1, c, i, p, x_all)
                xs_free(D1)(i, p)
                nc.vector.scalar_tensor_tensor(out=xs[:, p, :], in0=vbuf[:, p, :], scalar=SLOPE, in1=vbuf[:, p, :],
                                               op0=ALU.mult, op1=ALU.max).then_inc(D1.xs_ready.sem, 1)

            pipeline(dve, T, [(turn_evac(G[0]), 1), (row_max(G[0]), 0), (finish_d1, 1)])

            def out_free(i, p):
                dve.wait_ge(out_done[p].sem, (i - p) * 8 + 16)

            def finish_d2(i, p):
                c = Chain(dve, D2.fin_chain.sem, 5, i)
                if isinstance(i, int) and i == 0:
                    dve.wait_ge(D1.x_stored.sem, D1.x_stored.done(T))
                gat_out(D2, c, i, p, x1)
                c.link(nc.vector.scalar_tensor_tensor(out=vbuf[:, p, :], in0=vbuf[:, p, :], scalar=SLOPE, in1=vbuf[:, p, :],
                                                      op0=ALU.mult, op1=ALU.max))
                c.link(nc.vector.tensor_tensor(vbuf[:, p:p + 1, :], vbuf[:, p:p + 1, :], x_all[:, bass.ds(i, 1), :], ALU.add))
                norm(D2, i, p, c, out_free)

            pipeline(dve, T, [(turn_evac(G[1]), 1), (row_max(G[1]), 0), (finish_d2, 1)])

        @block.tensor
        def _(pe):
            credits(pe, adjT_turned, xw_ps, pos_ps, aggz_done, TC.turned, TD.turned)
            for ph in (A, B, C, D1, D2):
                credits(pe, ph.agg_done, ph.xs_turned, ph.proj_done)
            for g in G:
                credits(pe, g.scores_done, g.turned)
            pe.wait_ge(ident_ready.sem, 2)
            pe.wait_ge(w0_signed.sem, 1)
            w0T_v = bankb(7)[:, 0:KD * D].rearrange("p (k n) -> p k n", k=KD)
            for o in range(KD):
                for k in range(KD):
                    last = nc.tensor.transpose(w0T_v[:, k, o * P:(o + 1) * P], w0s[:, o, k * P:(k + 1) * P], identb[:, :])
            last.then_inc(w0T_ps.sem, 1)

            def pos_turn(i, p):
                pe.wait_ge(pos_ready.sem, i + 1)
                pe.wait_ge(posT_ready.sem, posT_ready.room(i))
                for k in range(KD):
                    last = nc.tensor.transpose(bankb(5 + p)[:, k * P:(k + 1) * P], pos[:, p, k * P:(k + 1) * P], identb[:, :])
                last.then_inc(pos_ps.sem, 1)

            def xw_mm(i, p):
                if isinstance(i, int) and i == 0:
                    pe.wait_ge(w0T_ready.sem, 1)
                pe.wait_ge(posT_ready.sem, posT_ready.done(i + 1))
                pe.wait_ge(xw_ready.sem, xw_ready.room(i))
                for k in range(KD):
                    last = nc.tensor.matmul(bank(3 + p, 0, D), posT[:, p, k, :], w0T[:, k, :], start=(k == 0), stop=(k == KD - 1))
                last.then_inc(xw_ps.sem, 1)

            pipeline(pe, T, [(pos_turn, 0), (xw_mm, 1)])

            def adj_turn(i, p):
                if isinstance(i, int) and i == FULL:
                    pe.wait_ge(adj_in_tail.sem, 32)
                else:
                    pe.wait_ge(adj_in[p].sem, (i - p) * 8 + 16)
                for g in range(BANKS_T):
                    pe.wait_ge(adjT_banks_read.sem, i * BANKS_T + g + 1)
                    for k in range(g * EB, min(g * EB + EB, T)):
                        last = nc.tensor.transpose(bank(g, (k % EB) * P, (k % EB) * P + P), adj_rows[:, p, k * P:(k + 1) * P],
                                                   ident[:, :])
                    last.then_inc(adjT_turned.sem, 1)

            def turn_x(ph, b, after=None):
                def stage(i, p):
                    pe.wait_ge(ph.xs_ready.sem, i + 1)
                    if after is None:
                        pe.wait_ge(ph.xT_ready.sem, ph.xT_ready.room(i))
                    else:
                        pe.wait_ge(after.WT_ready.sem, after.WT_ready.room(i))
                    for k in range(KD):
                        last = nc.tensor.transpose(bank(b, k * P, (k + 1) * P), xs[:, p, k * P:(k + 1) * P], ident[:, :])
                    last.then_inc(ph.xs_turned.sem, 1)
                return stage

            def agg_a(i, p):
                pe.wait_ge(lo_ready.sem, i + 1)
                if isinstance(i, int) and i == 0:
                    pe.wait_ge(xw_ready.sem, xw_ready.done(T))
                pe.wait_ge(A.xs_ready.sem, i - 1) if not (isinstance(i, int) and i < 2) else None
                for k in range(T):
                    for part in (hi, lo):
                        last = nc.tensor.matmul(bank(3 + p, 0, D), part[0:kk(k), p, k, :], xw[0:kk(k), k, :],
                                                start=(k == 0 and part is hi), stop=(k == T - 1 and part is lo))
                last.then_inc(A.agg_done.sem, 1)

            def proj_a(i, p):
                if isinstance(i, int) and i == 0:
                    pe.wait_ge(cols_ready.sem, 1)
                pe.wait_ge(A.xT_ready.sem, A.xT_ready.done(i + 1))
                pe.wait_ge(A.proj_ready.sem, A.proj_ready.room(i))
                for k in range(KD):
                    nc.tensor.matmul(bank(7), xTs[:, p, k, :], W1[:, k, :], start=(k == 0), stop=(k == KD - 1))
                for k in range(KD):
                    nc.tensor.matmul(bank(6, 0, 5), xTs[:, p, k, :], Wcol[:, k, 0:5], start=(k == 0), stop=(k == KD - 1))
                for k in range(KD):
                    last = nc.tensor.matmul(bank(6, P, 2 * P), WLb[:, k, :], xTs[:, p, k, :], start=(k == 0), stop=(k == KD - 1))
                last.then_inc(A.proj_done.sem, 1)

            pipeline(pe, T, [(turn_x(A, 5), 3), (adj_turn, 0), (proj_a, 3), (agg_a, 1)], apart=1)

            def agg_z(i, p):
                if isinstance(i, int) and i == 0:
                    pe.wait_ge(A.proj_ready.sem, A.proj_ready.done(T))
                pe.wait_ge(bprep_adj.sem, i + 1)
                if not (isinstance(i, int) and i < 2):
                    pe.wait_ge(gate_in_ready.sem, i - 1)
                for k in range(T):
                    last = nc.tensor.matmul(bank(p, 0, D + 2), adjTs[0:kk(k), p, k, :], feats[0:kk(k), k, 0, :],
                                            start=(k == 0), stop=(k == T - 1))
                last.then_inc(aggz_done.sem, 1)

            def agg_h(i, p):
                pe.wait_ge(bprep_exp.sem, i + 1)
                for k in range(T):
                    last = nc.tensor.matmul(bank(2 + p, 0, D + 1), eT[0:kk(k), p, k, :], feats[0:kk(k), k, 1, 0:D + 1],
                                            start=(k == 0), stop=(k == T - 1))
                last.then_inc(B.agg_done.sem, 1)

            def proj_b(i, p):
                pe.wait_ge(B.xT_ready.sem, B.xT_ready.done(i + 1))
                pe.wait_ge(B.proj_ready.sem, B.proj_ready.room(i))
                for k in range(KD):
                    last = nc.tensor.matmul(bank(7, 0, D), xTs[:, p, k, :], W2[:, k, :], start=(k == 0), stop=(k == KD - 1))
                last.then_inc(B.proj_done.sem, 1)

            pipeline(pe, T, [(turn_x(B, 5), 3), (agg_z, 1), (proj_b, 3), (agg_h, 1)])

            def agg_c(i, p):
                if isinstance(i, int) and i == 0:
                    pe.wait_ge(hid_chain.sem, 2 * T)
                pe.wait_ge(mask_ready.sem, i + 1)
                if not (isinstance(i, int) and i < 2):
                    pe.wait_ge(C.xs_ready.sem, i - 1)
                for k in range(T):
                    last = nc.tensor.matmul(bank(3 + p), maskT[0:kk(k), p, k, :], hid[0:kk(k), k, :],
                                            start=(k == 0), stop=(k == T - 1))
                last.then_inc(C.agg_done.sem, 1)

            def proj_d(ph, t, l):
                def stage(i, p):
                    pe.wait_ge(ph.xT_ready.sem, ph.xT_ready.done(i + 1))
                    pe.wait_ge(t.proj_s_ready.sem, t.proj_s_ready.room(i))
                    for k in range(KD):
                        last = nc.tensor.matmul(bank(7), xTs[:, p, k, :], W3[:, l, k, :], start=(k == 0), stop=(k == KD - 1))
                    last.then_inc(ph.proj_done.sem, 1)
                return stage

            def turn_w(t, b):
                def stage(i, p):
                    pe.wait_ge(t.proj_s_ready.sem, t.proj_s_ready.done(i + 1))
                    pe.wait_ge(t.WT_ready.sem, t.WT_ready.room(i))
                    for m in range(2 * KD):
                        last = nc.tensor.transpose(bank(b, m * P, (m + 1) * P), proj_s[:, p, m * P:(m + 1) * P], ident[:, :])
                    last.then_inc(t.turned.sem, 1)
                return stage

            pipeline(pe, T, [(turn_w(TC, 6), 4), (turn_x(C, 5), 3), (agg_c, 1), (proj_d(C, TC, 0), 3)])

            def scores(g, wt, t):
                def stage(i, p):
                    if isinstance(i, int) and i == 0:
                        pe.wait_ge(t.WT_ready.sem, t.WT_ready.done(T))
                    pe.wait_ge(g.WhTs_ready.sem, i + 1)
                    pe.wait_ge(g.probs_ready.sem, g.probs_ready.room(i))
                    for b, (c0, c1) in enumerate(CH):
                        for k in range(KD):
                            last = nc.tensor.matmul(bank(b, 0, c1 - c0), WhTs[:, p, k, :], wt[:, KD + k, c0:c1],
                                                    start=(k == 0), stop=(k == KD - 1))
                    last.then_inc(g.scores_done.sem, 1)
                return stage

            def turn_probs(g):
                def stage(i, p):
                    pe.wait_ge(pads_zero.sem, 2)
                    pe.wait_ge(g.probs_ready.sem, g.probs_ready.done(i + 1))
                    pe.wait_ge(g.probsT_ready.sem, g.probsT_ready.room(i))
                    for k in range(T):
                        last = nc.tensor.transpose(bank(3 + k // EB, (k % EB) * P, (k % EB) * P + P),
                                                   probs[:, p, k * P:(k + 1) * P], ident[:, :])
                    last.then_inc(g.turned.sem, 1)
                return stage

            def agg_d(ph, g, wh):
                def stage(i, p):
                    pe.wait_ge(g.probsT_ready.sem, g.probsT_ready.done(i + 1))
                    pe.wait_ge(ph.acc_read.sem, i + 2)
                    for k in range(T):
                        last = nc.tensor.matmul(bank(6, 0, D), probsT[0:kk(k), p, k, :], wh[0:kk(k), k, :],
                                                start=(k == 0), stop=(k == T - 1))
                    last.then_inc(ph.agg_done.sem, 1)
                return stage

            pipeline(pe, T, [(turn_probs(G[0]), 1), (turn_x(D1, 7, TD), 3), (scores(G[0], WT[0], TC), 0), (proj_d(D1, TD, 1), 3),
                             (agg_d(D1, G[0], Wh[0]), 1), (turn_w(TD, 7), 3)])
            pipeline(pe, T, [(turn_probs(G[1]), 1), (scores(G[1], WT[1], TD), 0), (agg_d(D2, G[1], Wh[1]), 1)])


_INS = ['x', 'adj', 'L0_gnn_weight', 'L1_gnn_W_sa', 'L1_gnn_a_sa', 'L1_gnn_W_gcnb', 'L1_gnn_b_gcnb', 'L1_gnn_Wa',
        'L1_gnn_ba', 'L1_gnn_Wb', 'L1_gnn_bb', 'L2_gnn_W', 'L2_gnn_b', 'L3_gnn_W_stack']


def kernel(**inputs):
    import numpy as _np
    import concourse.bacc as _bacc
    from concourse import mybir as _mybir
    from concourse.bass_utils import run_bass_kernel_spmd as _run

    nc = _bacc.Bacc("TRN2", target_bir_lowering=False, num_devices=1)
    arrays, args = {}, []
    for name in _INS:
        a = _np.ascontiguousarray(inputs[name])
        arrays[f"in_{name}_dram"] = a
        args.append(nc.dram_tensor(f"in_{name}_dram", a.shape, _mybir.dt.from_np(a.dtype), kind="ExternalInput").ap())
    out = nc.dram_tensor("out_0_dram", inputs["x"].shape, _mybir.dt.float32, kind="ExternalOutput").ap()
    gnn_stack(nc, *args, out)
    r = _run(nc, [arrays], core_ids=[0])
    return r.results[0]["out_0_dram"]
```

```python
from contextlib import ExitStack

import concourse.bass as bass
from concourse import mybir

F32 = mybir.dt.float32
BF16 = mybir.dt.bfloat16
ALU = mybir.AluOpType
ACT = mybir.ActivationFunctionType
AX = mybir.AxisListType

P = 128
BANK = 512
LN_EPS = 1e-5
ATTN_EPS = 1e-5
SLOPE = 0.01
MASKED = -3.0e38


class Count:

    def __init__(self, sem, credit=0):
        self.sem, self.credit = sem, credit

    def done(self, n):
        return n + self.credit

    def room(self, i):
        return i + 1


class Chain:

    def __init__(self, eng, sem, steps, i, taken=0):
        self.eng, self.sem, self.base, self.steps, self.n = eng, sem, i * steps, steps, taken

    def link(self, ins):
        self.n += 1
        assert self.n <= self.steps
        ins.then_inc(self.sem, 1)
        self.eng.wait_ge(self.sem, self.base + self.n)


def pipeline(eng, tiles, stages, apart=0, tail=None, left=(), extra=()):
    end = tiles - apart
    deep = max(lag for _, lag in stages)

    def step(s, parity, lo, hi):
        for stage, lag in stages:
            if lo - lag >= 0 and hi - lag < tiles:
                stage(s - lag, (parity - lag) % 2)

    first = deep + (end - deep) % 2
    for s in range(first):
        step(s, s % 2, s, s)
    with eng.Fori(0, (end - first) // 2) as turn:
        for d in range(2):
            step(turn * 2 + (first + d), (first + d) % 2, first, end - 1)
    if tail is None:
        for s in range(end, tiles + deep):
            step(s, s % 2, s, s)
    else:
        due = {(stage, i) for stage, lag in stages for i in range(end - lag, tiles)}
        assert due == (set(tail) | set(left)) - set(extra)
        for stage, i in tail:
            stage(i, i % 2)


def gnn_stack(nc, x, adj, w0, w_sa, a_sa, w_gcn, b_gcn, wa, ba, wb, bb, w2, b2, w3, out):
    N, D = x.shape
    T = -(-N // P)
    FULL = N // P
    TAIL = N - FULL * P
    NP = T * P
    KD = D // P
    assert D == 2 * P and T - FULL == 1 and w3.shape[0] == 2
    CH = [(c, min(c + BANK, N)) for c in range(0, N, BANK)]
    EB = BANK // P

    def kk(k):
        return P if k < FULL else TAIL

    ctx = ExitStack()
    with ctx:
        ctx.enter_context(nc.allow_non_contiguous_dma(reason="weight vectors as columns"))

        def sb(name, shape, dt=F32):
            return ctx.enter_context(nc.sbuf_tensor(name, shape, dt))

        def sem(name, credit=0):
            s = Count(ctx.enter_context(nc.semaphore(name)), credit)
            counts.append(s)
            return s

        counts = []

        adjT = sb("adjT", [P, T, NP])
        x_all = sb("x_all", [P, T, D])
        feats = sb("feats", [P, T, 2, D + 2])
        xs = sb("xs", [P, 2, D])
        xTs = sb("xTs", [P, 2, KD, P])
        vbuf = sb("vbuf", [P, 2, D])
        proj_s = sb("proj_s", [P, 2, 2 * D])
        WhTs = sb("WhTs", [P, 2, KD, P])
        ident = sb("ident", [P, P])
        identb = sb("identb", [P, P], BF16)
        W1 = sb("W1", [P, KD, 2 * D])
        Wcol = sb("Wcol", [P, KD, 6])
        nwl = sb("nwl", [P, KD])
        WLb = sb("WLb", [P, KD, P])
        W2 = sb("W2", [P, KD, D])
        W3 = sb("W3", [P, 2, KD, 2 * D])
        b1b = sb("b1b", [P, D])
        b2b = sb("b2b", [P, D])
        babb = sb("babb", [P, 2])
        hbab = sb("hbab", [P, 2])
        hattn = sb("hattn", [P, T, 2])
        nsr = sb("nsr", [P, T, 1])
        nsl = sb("nsl", [P, NP])
        deg = sb("deg", [P, T])
        rdeg = sb("rdeg", [P, T])
        pad_deg = sb("pad_deg", [P, T])
        nhalf = sb("nhalf", [P, 1])
        stats = sb("stats", [P, 2, 6])
        mv = sb("mv", [P, 2, 2])
        veps = sb("veps", [P, 2, 1])
        rstd = sb("rstd", [P, 2, 1])
        att_in = sb("att_in", [P, 2, 2])
        att_t = sb("att_t", [P, 2, 2])
        att = sb("att", [P, 2, 2])
        den = sb("den", [P, 2, 1])
        rden = sb("rden", [P, 2, 1])
        idle = sb("idle", [P, 1])
        negmax = sb("negmax", [P, 2, 1])
        esum = sb("esum", [P, 2, 1])

        SLOT = T * D * 4
        arena = sb("arena", [P, 7 * T * D])
        base = nc.sbuf_base - 7 * SLOT

        def at(name, slot, shape, dt=F32, skip=0):
            return nc.alloc_sbuf_tensor_at(name, shape, dt, offset=base + slot * SLOT + skip)

        adj_rows = at("adj_rows", 0, [P, 2, NP])
        HALF = SLOT // 2
        rest = at("rest", 1, [P, T, P])
        hi = at("hi", 2, [P, 2, T, P], BF16)
        mid = at("mid", 2, [P, 2, T, P], BF16, HALF)
        lo = at("lo", 3, [P, 2, T, P], BF16)
        xw = at("xw", 3, [P, T, D], BF16, HALF)
        adjTs = at("adjTs", 0, [P, 2, T, P])
        escore = at("escore", 1, [P, 2, T, P])
        eT = at("eT", 3, [P, 2, T, P])
        hid = at("hid", 4, [P, T, 3, D], BF16)
        maskT = at("maskT", 2, [P, 2, T, P], BF16)
        deg_mask = at("deg_mask", 2, [P, N], BF16, HALF)
        probs = at("probs", 2, [P, 2, NP])
        probsT = at("probsT", 3, [P, 2, T, P])
        WT = [at("WT0", 0, [P, 2 * KD, NP]), at("WT1", 4, [P, 2 * KD, NP])]
        x1 = at("x1", 6, [P, T, D])
        w0n = at("w0n", 4, [P, KD, D])
        KB = 2 * KD * D
        w0s = at("w0s", 6, [P, KD, D], BF16)
        w0neg = at("w0neg", 6, [P, KD, D], BF16, 2 * KB)
        w0T = at("w0T", 6, [P, KD, D], BF16, KB)
        pos = at("pos", 5, [P, T, D], BF16)
        posT = at("posT", 5, [P, KD, NP], BF16, HALF)
        a_b = at("a_b", 6, [P, 2 * D], F32, 4 * KB)
        dots = at("dots", 6, [P, D], F32, 8 * KB)
        hidden = at("hidden", 2, [P, D], F32, HALF)
        h_rest = at("h_rest", 2, [P, D], F32, HALF + 4 * D)

        psum = ctx.enter_context(nc.psum_tensor("psum", [P, 8, BANK], F32))
        Wh = [feats[:, :, 0, 0:D], feats[:, :, 1, 0:D]]

        def bank(b, lo_=0, hi_=BANK):
            return psum[:, b, lo_:hi_]

        def bankb(b):
            return psum[:, b, :].bitcast(BF16)

        adj_in_tail = sem("adj_in_tail")
        adj_in = [sem("adj_in_even"), sem("adj_in_odd")]
        x_in, w0_in, w_in, a_in, col_in = sem("x_in"), sem("w0_in"), sem("w_in"), sem("a_in"), sem("col_in")
        late_in = sem("late_in")
        pads_zero = sem("pads_zero")
        out_done = [sem("out_done_even", 16), sem("out_done_odd", 16)]
        dve_setup, consts_ready = sem("dve_setup"), sem("consts_ready")
        ident_ready, w0_signed, w0T_ps, w0T_ready = sem("ident_ready"), sem("w0_signed"), sem("w0T_ps"), sem("w0T_ready")
        cols_ready = sem("cols_ready")
        pos_ready, pos_ps, posT_ready, xw_ps, xw_ready = (
            sem("pos_ready"), sem("pos_ps"), sem("posT_ready"), sem("xw_ps"), sem("xw_ready"))

        class Phase:

            def __init__(s, n):
                s.agg_done = sem(n + "_agg_done", 2)
                s.acc_read = sem(n + "_acc_read", 2)
                s.fin_chain = sem(n + "_fin_chain")
                s.var_ready = sem(n + "_var_ready")
                s.rstd_ready = sem(n + "_rstd_ready")
                s.xs_ready = sem(n + "_xs_ready")
                s.x_stored = sem(n + "_x_stored", 2)
                s.xs_turned = sem(n + "_xs_turned", 2)
                s.xT_ready = sem(n + "_xT_ready", 1)
                s.proj_done = sem(n + "_proj_done", 2)
                s.proj_ready = sem(n + "_proj_ready", 1)

        A, B, C, D1, D2 = (Phase(n) for n in ("binary", "attn", "mean", "gat1", "gat2"))
        BANKS_T = -(-T // EB)
        adjT_turned = sem("adjT_turned", 2 * BANKS_T)
        adjT_banks_read = sem("adjT_banks_read", BANKS_T)
        rest_ready, mid_ready, lo_ready = sem("rest_ready"), sem("mid_ready"), sem("lo_ready")
        bprep_adj, bprep_mask, bprep_score, bprep_exp = (
            sem("stationary_adj_ready"), sem("mask_ready"), sem("score_ready"), sem("exp_ready"))
        aggz_done, score_chain, pool_chain = sem("aggz_done", 2), sem("score_chain"), sem("pool_chain")
        att_in_ready, att_ready, gate_in_ready, gate_ready = (
            sem("att_in_ready"), sem("att_ready"), sem("gate_in_ready"), sem("gate_ready"))
        deg_chain = sem("deg_chain")
        hid_chain = sem("hid_chain")
        mask_ready = sem("mean_mask_ready")

        class Gat:
            def __init__(s, n):
                s.WhTs_ready = sem(n + "_WhTs_ready")
                s.scores_done = sem(n + "_scores_done", 2)
                s.max_ready = sem(n + "_max_ready", 1)
                s.probs_ready = sem(n + "_probs_ready", 1)
                s.turned = sem(n + "_turned", 2)
                s.probsT_ready = sem(n + "_probsT_ready", 1)

        G = [Gat("g1"), Gat("g2")]

        class Turn:

            def __init__(s, n):
                s.proj_s_ready = sem(n + "_proj_s_ready", 1)
                s.turned = sem(n + "_WT_turned", 2)
                s.WT_ready = sem(n + "_WT_ready", 1)

        TC, TD = Turn("mean"), Turn("gat1")

        block = ctx.enter_context(nc.Block())

        def credits(eng, *cs):
            for c in cs:
                eng.sem_inc(c.sem, c.credit)

        @block.sync
        def _(sp):
            sp.dma_start(x_all[:, 0:FULL, :], x[0:FULL * P, :].rearrange("(t p) d -> p t d", p=P)).then_inc(x_in.sem, 16)
            sp.wait_ge(pads_zero.sem, 1)
            sp.dma_start(x_all[0:64, FULL, :], x[FULL * P:FULL * P + 64, :]).then_inc(x_in.sem, 16)
            sp.dma_start(x_all[64:TAIL, FULL, :], x[FULL * P + 64:N, :]).then_inc(x_in.sem, 16)

            def load_rows(i, p):
                sp.wait_ge(adjT_turned.sem, (i + 1) * BANKS_T)
                sp.dma_start(adj_rows[:, p, 0:N], adj[i * P:(i + 1) * P, :] if isinstance(i, int) else
                             adj[bass.ds(i * P, P), :]).then_inc(adj_in[p].sem, 16)

            with sp.Fori(0, FULL // 2) as pair:
                load_rows(pair * 2, 0)
                load_rows(pair * 2 + 1, 1)
            sp.wait_ge(adjT_turned.sem, (FULL + 1) * BANKS_T)
            sp.dma_start(adj_rows[0:64, 0, 0:N], adj[FULL * P:FULL * P + 64, :]).then_inc(adj_in_tail.sem, 16)
            sp.dma_start(adj_rows[64:TAIL, 0, 0:N], adj[FULL * P + 64:N, :]).then_inc(adj_in_tail.sem, 16)

            def store(i, p):
                sp.wait_ge(D2.xs_ready.sem, D2.xs_ready.done(i + 1))
                sp.dma_start(out[bass.ds(i * P, P), :], xs[:, p, :]).then_inc(out_done[p].sem, 16)

            with sp.Fori(0, FULL // 2) as pair:
                store(pair * 2, 0)
                store(pair * 2 + 1, 1)
            sp.wait_ge(D2.xs_ready.sem, D2.xs_ready.done(T))
            sp.dma_start(out[FULL * P:N, :], xs[0:TAIL, 0, :]).then_inc(out_done[0].sem, 16)
            sp.wait_ge(out_done[0].sem, 16 * (T + 1) // 2 + out_done[0].credit)
            sp.wait_ge(out_done[1].sem, 16 * (T // 2) + out_done[1].credit)

        @block.gpsimd
        def _(pool):
            credits(pool, A.x_stored, B.x_stored, C.x_stored, D1.x_stored)
            nc.gpsimd.memset(ident[:, :], 0.0).then_inc(pool_chain.sem, 1)
            nc.gpsimd.memset(identb[:, :], 0.0).then_inc(pool_chain.sem, 1)
            nc.gpsimd.memset(nhalf[:, :], -0.5).then_inc(consts_ready.sem, 1)
            pool.wait_ge(pool_chain.sem, 2)
            for m in (ident, identb):
                nc.gpsimd.affine_select(out=m[:, :], in_=m[:, :], compare_op=ALU.not_equal, fill=1.0, base=0,
                                        pattern=[[-1, P]], channel_multiplier=1).then_inc(ident_ready.sem, 1)
            pool.dma_start(a_b[:, :], a_sa.partition_broadcast(P).rearrange("p a d -> p (a d)")).then_inc(a_in.sem, 16)
            for n, w in enumerate((wa, wb)):
                for half in range(2):
                    for k in range(KD):
                        c = (half * KD + k) * P
                        pool.dma_start(Wcol[:, k, 2 * half + n:2 * half + n + 1],
                                       w[:, c:c + P].rearrange("a p -> p a")).then_inc(col_in.sem, 16)
            pool.dma_start(babb[:, 0:1], ba.partition_broadcast(P)).then_inc(col_in.sem, 16)
            pool.dma_start(babb[:, 1:2], bb.partition_broadcast(P)).then_inc(col_in.sem, 16)
            pool.dma_start(b1b[:, :], b_gcn.partition_broadcast(P)).then_inc(late_in.sem, 16)
            pool.dma_start(b2b[:, :], b2.partition_broadcast(P)).then_inc(late_in.sem, 16)
            pool.dma_start(W2[:, :, :], w2.rearrange("(k p) n -> p k n", p=P)).then_inc(late_in.sem, 16)
            for l in range(2):
                pool.dma_start(W3[:, l, :, :], w3[l].rearrange("(k p) n -> p k n", p=P)).then_inc(late_in.sem, 16)
            pool.wait_ge(consts_ready.sem, 1)

            def rsqrt(ph):
                def stage(i, p):
                    pool.wait_ge(ph.var_ready.sem, ph.var_ready.done(i + 1))
                    nc.gpsimd.tensor_tensor(rstd[:, p, :], veps[:, p, :], nhalf[:, :], ALU.pow).then_inc(ph.rstd_ready.sem, 1)
                return stage

            def store_x(ph, dst):
                def stage(i, p):
                    pool.wait_ge(ph.xs_ready.sem, ph.xs_ready.done(i + 1))
                    nc.gpsimd.tensor_copy(dst[:, bass.ds(i, 1), :], xs[:, p:p + 1, :]).then_inc(ph.x_stored.sem, 1)
                return stage

            pipeline(pool, T, [(rsqrt(A), 2), (store_x(A, x_all), 2)])

            pipeline(pool, T, [(rsqrt(B), 2), (store_x(B, x_all), 2)])
            pipeline(pool, T, [(rsqrt(C), 2), (store_x(C, x_all), 2)])

            def stage_WhT(g, t, wt):
                def stage(i, p):
                    pool.wait_ge(t.WT_ready.sem, t.WT_ready.done(i + 1))
                    pool.wait_ge(g.scores_done.sem, g.scores_done.room(i))
                    nc.gpsimd.tensor_copy(WhTs[:, p, :, :], wt[:, 0:KD, bass.ds(i * P, P)]).then_inc(g.WhTs_ready.sem, 1)
                return stage

            pipeline(pool, T, [(stage_WhT(G[0], TC, WT[0]), 0), (store_x(D1, x1), 2)])
            pipeline(pool, T, [(stage_WhT(G[1], TD, WT[1]), 0), (rsqrt(D2), 2)])

        @block.scalar
        def _(act):
            credits(act, A.xT_ready, B.xT_ready, C.xT_ready, D1.xT_ready, adjT_banks_read,
                    TC.proj_s_ready, TD.proj_s_ready, TC.WT_ready, TD.WT_ready, G[0].probs_ready, G[1].probs_ready)
            act.dma_start(w0n[:, :, :], w0.rearrange("(k p) d -> p k d", p=P)).then_inc(w0_in.sem, 16)
            act.dma_start(W1[:, :, 0:D], w_gcn.rearrange("(k p) n -> p k n", p=P)).then_inc(w_in.sem, 16)
            act.dma_start(W1[:, :, D:2 * D], w_sa.rearrange("(k p) n -> p k n", p=P)).then_inc(w_in.sem, 16)

            act.wait_ge(w0T_ps.sem, 1)
            nc.scalar.activation(w0T[:, :, :], bankb(7)[:, 0:KD * D].rearrange("p (k n) -> p k n", k=KD),
                                 ACT.Copy).then_inc(w0T_ready.sem, 1)

            for g in range(BANKS_T):
                t0, t1 = g * EB, min(g * EB + EB, T)
                act.wait_ge(pos_ps.sem, g + 1)
                nc.scalar.activation(posT[:, :, t0 * P:t1 * P],
                                     bankb(5 + g).rearrange("p (k n) -> p k n", k=KD)[:, :, 0:(t1 - t0) * P],
                                     ACT.Copy).then_inc(posT_ready.sem, 1)

            def xT_evac(ph, b):
                def stage(i, p):
                    act.wait_ge(ph.xs_turned.sem, ph.xs_turned.done(i + 1))
                    act.wait_ge(ph.proj_done.sem, ph.proj_done.room(i))
                    nc.scalar.activation(xTs[:, p, :, :], bank(b, 0, D).rearrange("p (k n) -> p k n", k=KD),
                                         ACT.Copy).then_inc(ph.xT_ready.sem, 1)
                return stage

            def adj_evac(i, p):
                act.wait_ge(A.agg_done.sem, A.agg_done.room(i))
                for g in range(BANKS_T):
                    k0, k1 = g * EB, min(g * EB + EB, T)
                    act.wait_ge(adjT_turned.sem, adjT_turned.done(i * BANKS_T + g + 1))
                    src = bank(g, 0, (k1 - k0) * P).rearrange("p (k n) -> p k n", n=P)
                    nc.scalar.activation(adjT[:, k0:k1, bass.ds(i * P, P)], src, ACT.Copy)
                    last = nc.scalar.activation(hi[:, p, k0:k1, :], src, ACT.Copy)
                    last.then_inc(adjT_banks_read.sem, 1)

            def middle_bits(i, p):
                act.wait_ge(rest_ready.sem, i + 1)
                act.wait_ge(A.agg_done.sem, A.agg_done.room(i))
                nc.scalar.activation(mid[:, p, :, :], rest[:, :, :], ACT.Copy).then_inc(mid_ready.sem, 1)

            pipeline(act, T, [(xT_evac(A, 5), 3), (adj_evac, 0), (middle_bits, 0)])

            def copy_adj(i, p):
                if isinstance(i, int) and i == 0:
                    act.wait_ge(adjT_turned.sem, adjT_turned.done(BANKS_T * T))
                act.wait_ge(aggz_done.sem, aggz_done.room(i))
                nc.scalar.activation(adjTs[:, p, :, :], adjT[:, :, bass.ds(i * P, P)], ACT.Copy).then_inc(bprep_adj.sem, 1)

            def exp_scores(i, p):
                act.wait_ge(bprep_score.sem, i + 1)
                act.wait_ge(B.agg_done.sem, B.agg_done.room(i))
                nc.scalar.activation(eT[:, p, :, :], escore[:, p, :, :], ACT.Exp).then_inc(bprep_exp.sem, 1)

            def gates(i, p):
                act.wait_ge(att_in_ready.sem, i + 1)
                nc.scalar.activation(att_t[:, p, :], att_in[:, p, :], ACT.Tanh).then_inc(att_ready.sem, 1)
                act.wait_ge(gate_in_ready.sem, i + 1)
                nc.scalar.activation(vbuf[:, p, :], vbuf[:, p, :], ACT.Tanh, scale=0.5).then_inc(gate_ready.sem, 1)

            xT_b = xT_evac(B, 5)
            pipeline(act, T, [(copy_adj, 0), (gates, 2), (xT_b, 3), (exp_scores, 0)],
                     tail=[(xT_b, T - 3), (gates, T - 2), (xT_b, T - 2), (gates, T - 1), (xT_b, T - 1)])

            def proj_evac(ph, t, wh):
                def stage(i, p):
                    act.wait_ge(ph.proj_done.sem, ph.proj_done.done(i + 1))
                    act.wait_ge(t.turned.sem, t.turned.room(i))
                    nc.scalar.activation(wh[:, bass.ds(i, 1), :], bank(7, 0, D).unsqueeze(1), ACT.Copy)
                    nc.scalar.activation(proj_s[:, p, :], bank(7), ACT.Copy).then_inc(t.proj_s_ready.sem, 1)
                return stage

            def WT_evac(t, wt, b):
                def stage(i, p):
                    act.wait_ge(t.turned.sem, t.turned.done(i + 1))
                    nc.scalar.activation(wt[:, :, bass.ds(i * P, P)], bank(b).rearrange("p (m n) -> p m n", n=P),
                                         ACT.Copy).then_inc(t.WT_ready.sem, 1)
                return stage

            xT_c, WT_c, proj_c = xT_evac(C, 5), WT_evac(TC, WT[0], 6), proj_evac(C, TC, Wh[0])
            pipeline(act, T, [(xT_c, 3), (WT_c, 4), (proj_c, 3)],
                     tail=[(xT_c, T - 3), (WT_c, T - 4), (proj_c, T - 3), (xT_c, T - 2), (WT_c, T - 3), (proj_c, T - 2),
                           (xT_c, T - 1), (WT_c, T - 2), (proj_c, T - 1), (WT_c, T - 1)])

            def exp_row(g):
                def stage(i, p):
                    act.wait_ge(g.max_ready.sem, g.max_ready.done(i + 1))
                    act.wait_ge(g.turned.sem, g.turned.room(i))
                    nc.scalar.activation(probs[:, p, 0:N], psum[:, 0:len(CH), :].rearrange("p b n -> p (b n)")[:, 0:N],
                                         ACT.Exp, bias=negmax[:, p, :], accum_out=esum[:, p, :]).then_inc(g.probs_ready.sem, 1)
                return stage

            pipeline(act, T, [(xT_evac(D1, 7), 3), (exp_row(G[0]), 0), (proj_evac(D1, TD, Wh[1]), 3), (WT_evac(TD, WT[1], 7), 3)])
            pipeline(act, T, [(exp_row(G[1]), 0)])

        @block.vector
        def _(dve):
            credits(dve, A.acc_read, B.acc_read, C.acc_read, D1.acc_read, D2.acc_read,
                    A.proj_ready, B.proj_ready, G[0].max_ready, G[1].max_ready, G[0].probsT_ready, G[1].probsT_ready)
            for o in out_done:
                dve.sem_inc(o.sem, o.credit)
            nc.vector.memset(x_all[:, FULL, :], 0.0).then_inc(dve_setup.sem, 1)
            dve.wait_ge(dve_setup.sem, 1)
            nc.vector.memset(adj_rows[:, :, N:NP], 0.0).then_inc(pads_zero.sem, 1)
            nc.vector.memset(feats[:, :, 1, D:D + 2], 1.0)
            nc.vector.memset(WLb[:, :, :], 0.0).then_inc(dve_setup.sem, 1)
            nc.vector.memset(pad_deg[:, :], 0.0).then_inc(dve_setup.sem, 1)
            dve.wait_ge(dve_setup.sem, 3)
            nc.vector.memset(pad_deg[:, FULL:T], 1.0).then_inc(dve_setup.sem, 1)
            dve.wait_ge(dve_setup.sem, 4)
            nc.vector.memset(pad_deg[0:TAIL, FULL:T], 0.0).then_inc(dve_setup.sem, 1)
            dve.wait_ge(w0_in.sem, 16)
            nc.vector.tensor_scalar(w0neg[:, :, :], w0n[:, :, :], 0.0, None, ALU.is_lt).then_inc(dve_setup.sem, 1)
            dve.wait_ge(dve_setup.sem, 6)
            nc.vector.scalar_tensor_tensor(out=w0s[:, :, :], in0=w0n[:, :, :], scalar=0.0, in1=w0neg[:, :, :],
                                           op0=ALU.is_gt, op1=ALU.subtract).then_inc(w0_signed.sem, 1)
            dve.wait_ge(x_in.sem, 48)

            nc.vector.tensor_scalar(pos[:, :, :], x_all[:, :, :], 0.0, None, ALU.is_gt).then_inc(pos_ready.sem, 1)
            for t0 in range(0, T, 2):
                t1 = min(t0 + 2, T)
                dve.wait_ge(xw_ps.sem, t0 // 2 + 1)
                nc.vector.tensor_copy(xw[:, t0:t1, :], bank(t0 // 2, 0, (t1 - t0) * D).rearrange("p (t n) -> p t n", n=D))\
                    .then_inc(xw_ready.sem, 1)

            dve.wait_ge(a_in.sem, 16)
            dve.wait_ge(w_in.sem, 16 * 2)
            dve.wait_ge(col_in.sem, 16 * 10)
            for half, dst in ((0, nwl), (1, None)):
                for k in range(KD):
                    acc = nwl[:, k:k + 1] if half == 0 else Wcol[:, k, 4:5]
                    nc.vector.tensor_tensor_reduce(out=dots[:, :], in0=W1[:, k, D:2 * D],
                                                   in1=a_b[:, half * D:(half + 1) * D], scale=-1.0, scalar=0.0,
                                                   op0=ALU.mult, op1=ALU.add, accum_out=acc).then_inc(dve_setup.sem, 1)
                    dve.wait_ge(dve_setup.sem, 7 + half * KD + k)
            for k in range(KD):
                nc.vector.tensor_scalar(WLb[:, k, :], WLb[:, k, :], nwl[:, k:k + 1], None, ALU.add)
            nc.vector.tensor_scalar(hbab[:, :], babb[:, :], 0.5, None, ALU.mult).then_inc(cols_ready.sem, 1)
            dve.wait_ge(cols_ready.sem, 1)

            def norm_stats(ph, i, p, c):
                c.link(nc.vector.bn_stats(stats[:, p, :], vbuf[:, p, :]))
                nc.vector.memset(idle[:, :], 0.0)
                c.link(nc.vector.bn_aggr(mv[:, p, :], stats[:, p, :]))
                nc.vector.tensor_scalar(veps[:, p, :], mv[:, p, 1:2], LN_EPS, None, ALU.add).then_inc(ph.var_ready.sem, 1)

            def norm_apply(ph, free):
                def stage(i, p):
                    free(i, p)
                    dve.wait_ge(ph.rstd_ready.sem, i + 1)
                    nc.vector.tensor_scalar(xs[:, p, :], vbuf[:, p, :], mv[:, p, 0:1], rstd[:, p, :], ALU.subtract,
                                            ALU.mult).then_inc(ph.xs_ready.sem, 1)
                return stage

            def xs_free(ph):
                def free(i, p):
                    dve.wait_ge(ph.xs_turned.sem, ph.xs_turned.room(i))
                    dve.wait_ge(ph.x_stored.sem, ph.x_stored.room(i))
                return free

            def rest_bits(i, p):
                if isinstance(i, int) and i == 0:
                    pass
                else:
                    dve.wait_ge(lo_ready.sem, i)
                for g in range(BANKS_T):
                    k0, k1 = g * EB, min(g * EB + EB, T)
                    dve.wait_ge(adjT_banks_read.sem, adjT_banks_read.done(BANKS_T * i + g + 1))
                    last = nc.vector.tensor_tensor(rest[:, k0:k1, :], adjT[:, k0:k1, bass.ds(i * P, P)], hi[:, p, k0:k1, :],
                                                   ALU.subtract)
                last.then_inc(rest_ready.sem, 1)

            def lower_bits(i, p):
                dve.wait_ge(mid_ready.sem, i + 1)
                nc.vector.tensor_tensor(lo[:, p, :, :], rest[:, :, :], mid[:, p, :, :], ALU.subtract).then_inc(lo_ready.sem, 1)

            def finish_a(i, p):
                c = Chain(dve, A.fin_chain.sem, 3, i)
                dve.wait_ge(A.agg_done.sem, A.agg_done.done(i + 1))
                ins = nc.vector.scalar_tensor_tensor(out=vbuf[:, p:p + 1, :], in0=bank(3 + p, 0, D).unsqueeze(1), scalar=0.0,
                                                     in1=x_all[:, bass.ds(i, 1), :], op0=ALU.max, op1=ALU.add)
                c.link(ins)
                norm_stats(A, i, p, c)

            def evac_a(i, p):
                dve.wait_ge(A.proj_done.sem, A.proj_done.done(i + 1))
                nc.vector.tensor_copy(feats[:, bass.ds(i, 1), :, 0:D],
                                      bank(7).rearrange("p (a b n) -> p a b n", a=1, b=2))
                nc.vector.tensor_copy(feats[:, bass.ds(i, 1), 0:1, D:D + 2], bank(6, 0, 2).unsqueeze(1).unsqueeze(1))
                nc.vector.scalar_tensor_tensor(out=hattn[:, bass.ds(i, 1), :], in0=bank(6, 2, 4).unsqueeze(1), scalar=0.5,
                                               in1=hbab[:, :].unsqueeze(1), op0=ALU.mult, op1=ALU.add)
                nc.vector.tensor_copy(nsr[:, bass.ds(i, 1), :], bank(6, 4, 5).unsqueeze(1))
                nc.vector.tensor_copy(nsl[:, bass.ds(i * P, P)], bank(6, P, 2 * P)).then_inc(A.proj_ready.sem, 1)

            apply_a = norm_apply(A, xs_free(A))
            pipeline(dve, T, [(finish_a, 2), (rest_bits, 0), (apply_a, 2), (evac_a, 3), (lower_bits, 0)],
                     tail=[(finish_a, T - 2), (apply_a, T - 2), (evac_a, T - 3), (finish_a, T - 1), (apply_a, T - 1), (evac_a, T - 2)],
                     left=[(evac_a, T - 1)])

            def mask_b(i, p):
                c = Chain(dve, score_chain.sem, 2, i)
                dve.wait_ge(B.agg_done.sem, B.agg_done.room(i))
                c.link(nc.vector.tensor_scalar(escore[:, p, :, :], adjT[:, :, bass.ds(i * P, P)], 0.0, MASKED, ALU.is_equal,
                                               ALU.mult))

            def add_scores(i, p, ks):
                for k in ks:
                    last = nc.vector.scalar_tensor_tensor(out=escore[:, p, k, :], in0=escore[:, p, k, :], scalar=nsr[:, k, :],
                                                          in1=nsl[:, bass.ds(i * P, P)], op0=ALU.add, op1=ALU.add)
                return last

            def scores_b(i, p):
                mask_b(i, p)
                if isinstance(i, int) and i == 0:
                    dve.wait_ge(A.proj_ready.sem, A.proj_ready.done(FULL))
                    add_scores(i, p, range(FULL))
                    evac_a(T - 1, (T - 1) % 2)
                    dve.wait_ge(A.proj_ready.sem, A.proj_ready.done(T))
                    last = add_scores(i, p, [FULL])
                else:
                    last = add_scores(i, p, range(T))
                Chain(dve, score_chain.sem, 2, i, 1).link(last)
                nc.vector.scalar_tensor_tensor(out=escore[:, p, :, :], in0=escore[:, p, :, :], scalar=SLOPE,
                                               in1=escore[:, p, :, :], op0=ALU.mult, op1=ALU.min).then_inc(bprep_score.sem, 1)

            def finish_b(i, p):
                c = Chain(dve, B.fin_chain.sem, 10, i)
                dve.wait_ge(aggz_done.sem, aggz_done.done(i + 1))
                nc.vector.scalar_tensor_tensor(out=att_in[:, p:p + 1, :], in0=bank(p, D, D + 2).unsqueeze(1), scalar=0.5,
                                               in1=hattn[:, bass.ds(i, 1), :], op0=ALU.mult, op1=ALU.add).then_inc(att_in_ready.sem, 1)
                c.link(nc.vector.tensor_tensor(vbuf[:, p, :], bank(p, 0, D), b1b[:, :], ALU.add))
                dve.wait_ge(att_ready.sem, i + 1)
                c.link(nc.vector.tensor_scalar(att[:, p, :], att_t[:, p, :], 0.5, 0.5, ALU.mult, ALU.add))
                c.link(nc.vector.tensor_scalar(vbuf[:, p, :], vbuf[:, p, :], att[:, p, 1:2], None, ALU.mult))
                dve.wait_ge(B.agg_done.sem, B.agg_done.done(i + 1))
                c.link(nc.vector.tensor_scalar(den[:, p, :], bank(2 + p, D, D + 1), ATTN_EPS, None, ALU.add))
                c.link(nc.vector.reciprocal(rden[:, p, :], den[:, p, :]))
                c.link(nc.vector.tensor_tensor(rden[:, p, :], rden[:, p, :], att[:, p, 0:1], ALU.mult))
                nc.vector.scalar_tensor_tensor(out=vbuf[:, p, :], in0=bank(2 + p, 0, D), scalar=rden[:, p, :], in1=vbuf[:, p, :],
                                               op0=ALU.mult, op1=ALU.add).then_inc(gate_in_ready.sem, 1)

            def finish_b2(i, p):
                c = Chain(dve, B.fin_chain.sem, 10, i, 6)
                dve.wait_ge(gate_ready.sem, i + 1)
                c.link(nc.vector.tensor_scalar(vbuf[:, p, :], vbuf[:, p, :], 0.5, 0.5, ALU.mult, ALU.add))
                c.link(nc.vector.tensor_tensor(vbuf[:, p:p + 1, :], vbuf[:, p:p + 1, :], x_all[:, bass.ds(i, 1), :], ALU.add))
                norm_stats(B, i, p, c)

            def evac_b(i, p):
                c = Chain(dve, hid_chain.sem, 4, i)
                dve.wait_ge(B.proj_done.sem, B.proj_done.done(i + 1))
                nc.vector.tensor_tensor(hidden[:, :], bank(7, 0, D), b2b[:, :], ALU.add).then_inc(B.proj_ready.sem, 1)
                dve.wait_ge(B.proj_ready.sem, B.proj_ready.done(i + 1))
                whole, rest_h = hidden[:, :].unsqueeze(1), h_rest[:, :].unsqueeze(1)
                c.link(nc.vector.tensor_copy(hid[:, bass.ds(i, 1), 0, :], whole))
                c.link(nc.vector.tensor_tensor(rest_h, whole, hid[:, bass.ds(i, 1), 0, :], ALU.subtract))
                c.link(nc.vector.tensor_copy(hid[:, bass.ds(i, 1), 1, :], rest_h))
                c.link(nc.vector.tensor_tensor(hid[:, bass.ds(i, 1), 2, :], rest_h, hid[:, bass.ds(i, 1), 1, :], ALU.subtract))

            def mask_tile(i, p):
                nc.vector.tensor_scalar(maskT[:, p, :, :], adjT[:, :, bass.ds(i * P, P)], 0.0, None,
                                        ALU.not_equal).then_inc(mask_ready.sem, 1)

            def mask(i, p):
                if isinstance(i, int) and i == 0:
                    return
                dve.wait_ge(C.agg_done.sem, C.agg_done.room(i))
                mask_tile(i, p)

            dve.wait_ge(late_in.sem, 16 * 5)
            apply_b = norm_apply(B, xs_free(B))
            pipeline(dve, T, [(finish_b, 2), (scores_b, 0), (finish_b2, 2), (evac_b, 3), (apply_b, 2)],
                     tail=[(finish_b, T - 2), (finish_b2, T - 2), (apply_b, T - 2), (evac_b, T - 3), (mask_tile, 0), (evac_b, T - 2),
                           (finish_b, T - 1), (finish_b2, T - 1), (apply_b, T - 1), (evac_b, T - 1)], extra=[(mask_tile, 0)])

            def degree(i, p):
                c = Chain(dve, deg_chain.sem, 3, i)
                d = deg[:, bass.ds(i, 1)]
                c.link(nc.vector.tensor_scalar(deg_mask[:, :].unsqueeze(1), adjT[:, bass.ds(i, 1), 0:N], 0.0, 0.0,
                                               ALU.not_equal, ALU.add, accum_out=d))
                c.link(nc.vector.tensor_tensor(d, d, pad_deg[:, bass.ds(i, 1)], ALU.add))
                c.link(nc.vector.reciprocal(rdeg[:, bass.ds(i, 1)], d))

            def finish_c(i, p):
                c = Chain(dve, C.fin_chain.sem, 3, i)
                dve.wait_ge(C.agg_done.sem, C.agg_done.done(i + 1))
                r = rdeg[:, bass.ds(i, 1)]
                c.link(nc.vector.scalar_tensor_tensor(out=vbuf[:, p:p + 1, :], in0=bank(3 + p, 0, D).unsqueeze(1), scalar=r,
                                                      in1=x_all[:, bass.ds(i, 1), :], op0=ALU.mult, op1=ALU.add))
                norm_stats(C, i, p, c)

            apply_c = norm_apply(C, xs_free(C))
            pipeline(dve, T, [(finish_c, 2), (mask, 0), (apply_c, 2), (degree, 0)])

            nc.vector.memset(probs[:, :, N:NP], 0.0).then_inc(pads_zero.sem, 1)

            def turn_evac(g):
                def stage(i, p):
                    dve.wait_ge(g.turned.sem, g.turned.done(i + 1))
                    nc.vector.tensor_tensor(probsT[:, p, :, :], psum[:, 3:3 + BANKS_T, :].rearrange("p b (k n) -> p (b k) n", n=P)[:, 0:T, :],
                                            adjT[:, :, bass.ds(i * P, P)], ALU.mult).then_inc(g.probsT_ready.sem, 1)
                return stage

            def row_max(g):
                def stage(i, p):
                    dve.wait_ge(g.scores_done.sem, g.scores_done.done(i + 1))
                    nc.vector.tensor_reduce(negmax[:, p, :], psum[:, 0:len(CH), :].rearrange("p b n -> p (b n)")[:, 0:N], AX.X,
                                            ALU.max, negate=True).then_inc(g.max_ready.sem, 1)
                return stage

            def gat_out(ph, c, i, p, xin):
                dve.wait_ge(ph.agg_done.sem, ph.agg_done.done(i + 1))
                c.link(nc.vector.reciprocal(rden[:, p, :], esum[:, p, :]))
                ins = nc.vector.scalar_tensor_tensor(out=vbuf[:, p:p + 1, :], in0=bank(6, 0, D).unsqueeze(1), scalar=rden[:, p, :],
                                                     in1=xin[:, bass.ds(i, 1), :], op0=ALU.mult, op1=ALU.add)
                ins.then_inc(ph.acc_read.sem, 1)
                dve.wait_ge(ph.acc_read.sem, ph.acc_read.done(i + 1))

            def finish_d1(i, p):
                c = Chain(dve, D1.fin_chain.sem, 1, i)
                gat_out(D1, c, i, p, x_all)
                xs_free(D1)(i, p)
                nc.vector.scalar_tensor_tensor(out=xs[:, p, :], in0=vbuf[:, p, :], scalar=SLOPE, in1=vbuf[:, p, :],
                                               op0=ALU.mult, op1=ALU.max).then_inc(D1.xs_ready.sem, 1)

            pipeline(dve, T, [(turn_evac(G[0]), 1), (row_max(G[0]), 0), (finish_d1, 1)])

            def out_free(i, p):
                dve.wait_ge(out_done[p].sem, (i - p) * 8 + 16)

            def finish_d2(i, p):
                c = Chain(dve, D2.fin_chain.sem, 5, i)
                if isinstance(i, int) and i == 0:
                    dve.wait_ge(D1.x_stored.sem, D1.x_stored.done(T))
                gat_out(D2, c, i, p, x1)
                c.link(nc.vector.scalar_tensor_tensor(out=vbuf[:, p, :], in0=vbuf[:, p, :], scalar=SLOPE, in1=vbuf[:, p, :],
                                                      op0=ALU.mult, op1=ALU.max))
                c.link(nc.vector.tensor_tensor(vbuf[:, p:p + 1, :], vbuf[:, p:p + 1, :], x_all[:, bass.ds(i, 1), :], ALU.add))
                norm_stats(D2, i, p, c)

            apply_d = norm_apply(D2, out_free)
            pipeline(dve, T, [(turn_evac(G[1]), 1), (row_max(G[1]), 0), (finish_d2, 1), (apply_d, 1)])

        @block.tensor
        def _(pe):
            credits(pe, adjT_turned, aggz_done, TC.turned, TD.turned)
            for ph in (A, B, C, D1, D2):
                credits(pe, ph.agg_done, ph.xs_turned, ph.proj_done)
            for g in G:
                credits(pe, g.scores_done, g.turned)
            pe.wait_ge(ident_ready.sem, 2)
            pe.wait_ge(w0_signed.sem, 1)
            w0T_v = bankb(7)[:, 0:KD * D].rearrange("p (k n) -> p k n", k=KD)
            for o in range(KD):
                for k in range(KD):
                    last = nc.tensor.transpose(w0T_v[:, k, o * P:(o + 1) * P], w0s[:, o, k * P:(k + 1) * P], identb[:, :])
            last.then_inc(w0T_ps.sem, 1)

            pe.wait_ge(pos_ready.sem, 1)
            pe.wait_ge(w0T_ready.sem, 1)
            for g in range(BANKS_T):
                t0, t1 = g * EB, min(g * EB + EB, T)
                for t in range(t0, t1):
                    for k in range(KD):
                        c = k * EB * P + (t - t0) * P
                        last = nc.tensor.transpose(bankb(5 + g)[:, c:c + P], pos[:, t, k * P:(k + 1) * P], identb[:, :])
                last.then_inc(pos_ps.sem, 1)
            for t in range(T):
                if t % EB == 0:
                    pe.wait_ge(posT_ready.sem, t // EB + 1)
                for k in range(KD):
                    last = nc.tensor.matmul(bank(t // 2, (t % 2) * D, (t % 2 + 1) * D), posT[:, k, t * P:(t + 1) * P], w0T[:, k, :],
                                            start=(k == 0), stop=(k == KD - 1))
                if t % 2 or t == T - 1:
                    last.then_inc(xw_ps.sem, 1)
            pe.wait_ge(xw_ready.sem, -(-T // 2))

            def adj_turn(i, p):
                if isinstance(i, int) and i == FULL:
                    pe.wait_ge(adj_in_tail.sem, 32)
                else:
                    pe.wait_ge(adj_in[p].sem, (i - p) * 8 + 16)
                for g in range(BANKS_T):
                    pe.wait_ge(adjT_banks_read.sem, i * BANKS_T + g + 1)
                    for k in range(g * EB, min(g * EB + EB, T)):
                        last = nc.tensor.transpose(bank(g, (k % EB) * P, (k % EB) * P + P), adj_rows[:, p, k * P:(k + 1) * P],
                                                   ident[:, :])
                    last.then_inc(adjT_turned.sem, 1)

            def turn_x(ph, b, after=None):
                def stage(i, p):
                    pe.wait_ge(ph.xs_ready.sem, i + 1)
                    if after is None:
                        pe.wait_ge(ph.xT_ready.sem, ph.xT_ready.room(i))
                    else:
                        pe.wait_ge(after.WT_ready.sem, after.WT_ready.room(i))
                    for k in range(KD):
                        last = nc.tensor.transpose(bank(b, k * P, (k + 1) * P), xs[:, p, k * P:(k + 1) * P], ident[:, :])
                    last.then_inc(ph.xs_turned.sem, 1)
                return stage

            def agg_a(i, p):
                pe.wait_ge(lo_ready.sem, i + 1)
                if isinstance(i, int) and i == 0:
                    pe.wait_ge(xw_ready.sem, -(-T // 2))
                if not (isinstance(i, int) and i < 2):
                    pe.wait_ge(A.xs_ready.sem, i - 1)
                for k in range(T):
                    for part in (hi, mid, lo):
                        last = nc.tensor.matmul(bank(3 + p, 0, D), part[0:kk(k), p, k, :], xw[0:kk(k), k, :],
                                                start=(k == 0 and part is hi), stop=(k == T - 1 and part is lo))
                last.then_inc(A.agg_done.sem, 1)

            def proj_a(i, p):
                if isinstance(i, int) and i == 0:
                    pe.wait_ge(cols_ready.sem, 1)
                pe.wait_ge(A.xT_ready.sem, A.xT_ready.done(i + 1))
                pe.wait_ge(A.proj_ready.sem, A.proj_ready.room(i))
                for k in range(KD):
                    nc.tensor.matmul(bank(7), xTs[:, p, k, :], W1[:, k, :], start=(k == 0), stop=(k == KD - 1))
                for k in range(KD):
                    nc.tensor.matmul(bank(6, 0, 5), xTs[:, p, k, :], Wcol[:, k, 0:5], start=(k == 0), stop=(k == KD - 1))
                for k in range(KD):
                    last = nc.tensor.matmul(bank(6, P, 2 * P), WLb[:, k, :], xTs[:, p, k, :], start=(k == 0), stop=(k == KD - 1))
                last.then_inc(A.proj_done.sem, 1)

            pipeline(pe, T, [(turn_x(A, 5), 3), (adj_turn, 0), (proj_a, 3), (agg_a, 1)], apart=1)

            def agg_z(i, p):
                if isinstance(i, int) and i == 0:
                    pe.wait_ge(A.proj_ready.sem, A.proj_ready.done(FULL))
                pe.wait_ge(bprep_adj.sem, i + 1)
                if not (isinstance(i, int) and i < 2):
                    pe.wait_ge(gate_in_ready.sem, i - 1)
                for k in range(T):
                    if k == FULL and isinstance(i, int) and i == 0:
                        pe.wait_ge(A.proj_ready.sem, A.proj_ready.done(T))
                    last = nc.tensor.matmul(bank(p, 0, D + 2), adjTs[0:kk(k), p, k, :], feats[0:kk(k), k, 0, :],
                                            start=(k == 0), stop=(k == T - 1))
                last.then_inc(aggz_done.sem, 1)

            def agg_h(i, p):
                pe.wait_ge(bprep_exp.sem, i + 1)
                for k in range(T):
                    last = nc.tensor.matmul(bank(2 + p, 0, D + 1), eT[0:kk(k), p, k, :], feats[0:kk(k), k, 1, 0:D + 1],
                                            start=(k == 0), stop=(k == T - 1))
                last.then_inc(B.agg_done.sem, 1)

            def proj_b(i, p):
                pe.wait_ge(B.xT_ready.sem, B.xT_ready.done(i + 1))
                pe.wait_ge(B.proj_ready.sem, B.proj_ready.room(i))
                for k in range(KD):
                    last = nc.tensor.matmul(bank(7, 0, D), xTs[:, p, k, :], W2[:, k, :], start=(k == 0), stop=(k == KD - 1))
                last.then_inc(B.proj_done.sem, 1)

            def agg_c(i, p, ks=None):
                first_tile = isinstance(i, int) and i == 0
                pe.wait_ge(mask_ready.sem, i + 1)
                if not (isinstance(i, int) and i < 2):
                    pe.wait_ge(C.xs_ready.sem, i - 1)
                if first_tile and ks is None:
                    ks = range(T - 3, T)
                for k in range(T) if ks is None else ks:
                    if first_tile:
                        pe.wait_ge(hid_chain.sem, 4 * (k + 1))
                    for part in range(3):
                        last = nc.tensor.matmul(bank(3 + p, 0, D), maskT[0:kk(k), p, k, :], hid[0:kk(k), k, part, :],
                                                start=(k == 0 and part == 0), stop=(k == T - 1 and part == 2))
                if k == T - 1:
                    last.then_inc(C.agg_done.sem, 1)

            turn_b = turn_x(B, 5)

            def agg_c_start(i, p):
                agg_c(0, 0, range(T - 3))

            pipeline(pe, T, [(turn_b, 3), (agg_z, 1), (proj_b, 3), (agg_h, 1)],
                     tail=[(turn_b, T - 3), (agg_z, T - 1), (proj_b, T - 3), (agg_h, T - 1), (turn_b, T - 2), (proj_b, T - 2),
                           (agg_c_start, 0), (turn_b, T - 1), (proj_b, T - 1)], extra=[(agg_c_start, 0)])

            def proj_d(ph, t, l):
                def stage(i, p):
                    pe.wait_ge(ph.xT_ready.sem, ph.xT_ready.done(i + 1))
                    pe.wait_ge(t.proj_s_ready.sem, t.proj_s_ready.room(i))
                    for k in range(KD):
                        last = nc.tensor.matmul(bank(7), xTs[:, p, k, :], W3[:, l, k, :], start=(k == 0), stop=(k == KD - 1))
                    last.then_inc(ph.proj_done.sem, 1)
                return stage

            def turn_w(t, b):
                def stage(i, p):
                    pe.wait_ge(t.proj_s_ready.sem, t.proj_s_ready.done(i + 1))
                    pe.wait_ge(t.WT_ready.sem, t.WT_ready.room(i))
                    for m in range(2 * KD):
                        last = nc.tensor.transpose(bank(b, m * P, (m + 1) * P), proj_s[:, p, m * P:(m + 1) * P], ident[:, :])
                    last.then_inc(t.turned.sem, 1)
                return stage

            class scores:

                def __init__(self, g, wt, t):
                    self.g, self.wt, self.t = g, wt, t

                def chunk(self, b, i, p):
                    c0, c1 = CH[b]
                    if isinstance(i, int) and i == 0:
                        self_last = min(-(-c1 // P), T)
                        pe.wait_ge(self.t.WT_ready.sem, self.t.WT_ready.done(self_last))
                    for k in range(KD):
                        last = nc.tensor.matmul(bank(b, 0, c1 - c0), WhTs[:, p, k, :], self.wt[:, KD + k, c0:c1],
                                                start=(k == 0), stop=(k == KD - 1))
                    return last

                def start0(self, i, p):
                    pe.wait_ge(self.g.WhTs_ready.sem, 1)
                    self.chunk(0, 0, 0)

                def start1(self, i, p):
                    self.chunk(1, 0, 0)

                def __call__(self, i, p):
                    if isinstance(i, int) and i == 0:
                        self.chunk(2, i, p).then_inc(self.g.scores_done.sem, 1)
                        return
                    pe.wait_ge(self.g.WhTs_ready.sem, i + 1)
                    pe.wait_ge(self.g.probs_ready.sem, self.g.probs_ready.room(i))
                    for b in range(len(CH)):
                        last = self.chunk(b, i, p)
                    last.then_inc(self.g.scores_done.sem, 1)

            turn_xc, turn_wc, proj_c = turn_x(C, 5), turn_w(TC, 6), proj_d(C, TC, 0)
            scores_1 = scores(G[0], WT[0], TC)
            pipeline(pe, T, [(turn_xc, 3), (agg_c, 1), (turn_wc, 4), (proj_c, 3)],
                     tail=[(turn_xc, T - 3), (agg_c, T - 1), (turn_wc, T - 4), (proj_c, T - 3), (turn_xc, T - 2), (turn_wc, T - 3),
                           (proj_c, T - 2), (turn_xc, T - 1), (turn_wc, T - 2), (scores_1.start0, 0), (proj_c, T - 1),
                           (scores_1.start1, 0), (turn_wc, T - 1)], extra=[(scores_1.start0, 0), (scores_1.start1, 0)])

            def turn_probs(g):
                def stage(i, p):
                    pe.wait_ge(pads_zero.sem, 2)
                    pe.wait_ge(g.probs_ready.sem, g.probs_ready.done(i + 1))
                    pe.wait_ge(g.probsT_ready.sem, g.probsT_ready.room(i))
                    for k in range(T):
                        last = nc.tensor.transpose(bank(3 + k // EB, (k % EB) * P, (k % EB) * P + P),
                                                   probs[:, p, k * P:(k + 1) * P], ident[:, :])
                    last.then_inc(g.turned.sem, 1)
                return stage

            def agg_d(ph, g, wh):
                def stage(i, p):
                    pe.wait_ge(g.probsT_ready.sem, g.probsT_ready.done(i + 1))
                    pe.wait_ge(ph.acc_read.sem, i + 2)
                    for k in range(T):
                        last = nc.tensor.matmul(bank(6, 0, D), probsT[0:kk(k), p, k, :], wh[0:kk(k), k, :],
                                                start=(k == 0), stop=(k == T - 1))
                    last.then_inc(ph.agg_done.sem, 1)
                return stage

            turn_xd, turn_wd, proj_d1 = turn_x(D1, 7, TD), turn_w(TD, 7), proj_d(D1, TD, 1)
            turn_p1, agg_d1 = turn_probs(G[0]), agg_d(D1, G[0], Wh[0])
            scores_2 = scores(G[1], WT[1], TD)
            pipeline(pe, T, [(turn_p1, 1), (turn_xd, 3), (scores_1, 0), (proj_d1, 3), (agg_d1, 1), (turn_wd, 3)],
                     tail=[(turn_p1, T - 1), (turn_xd, T - 3), (proj_d1, T - 3), (agg_d1, T - 1), (turn_wd, T - 3),
                           (turn_xd, T - 2), (scores_2.start0, 0), (proj_d1, T - 2), (turn_wd, T - 2),
                           (turn_xd, T - 1), (proj_d1, T - 1), (scores_2.start1, 0), (turn_wd, T - 1)],
                     extra=[(scores_2.start0, 0), (scores_2.start1, 0)])
            pipeline(pe, T, [(turn_probs(G[1]), 1), (scores_2, 0), (agg_d(D2, G[1], Wh[1]), 1)])


_INS = ['x', 'adj', 'L0_gnn_weight', 'L1_gnn_W_sa', 'L1_gnn_a_sa', 'L1_gnn_W_gcnb', 'L1_gnn_b_gcnb', 'L1_gnn_Wa',
        'L1_gnn_ba', 'L1_gnn_Wb', 'L1_gnn_bb', 'L2_gnn_W', 'L2_gnn_b', 'L3_gnn_W_stack']


def kernel(**inputs):
    import numpy as _np
    import concourse.bacc as _bacc
    from concourse import mybir as _mybir
    from concourse.bass_utils import run_bass_kernel_spmd as _run

    nc = _bacc.Bacc("TRN2", target_bir_lowering=False, num_devices=1)
    arrays, args = {}, []
    for name in _INS:
        a = _np.ascontiguousarray(inputs[name])
        arrays[f"in_{name}_dram"] = a
        args.append(nc.dram_tensor(f"in_{name}_dram", a.shape, _mybir.dt.from_np(a.dtype), kind="ExternalInput").ap())
    out = nc.dram_tensor("out_0_dram", inputs["x"].shape, _mybir.dt.float32, kind="ExternalOutput").ap()
    gnn_stack(nc, *args, out)
    r = _run(nc, [arrays], core_ids=[0])
    return r.results[0]["out_0_dram"]
```

```python
from contextlib import ExitStack

import concourse.bass as bass
from concourse import mybir

F32 = mybir.dt.float32
BF16 = mybir.dt.bfloat16
ALU = mybir.AluOpType
ACT = mybir.ActivationFunctionType
AX = mybir.AxisListType

P = 128
BANK = 512
LN_EPS = 1e-5
ATTN_EPS = 1e-5
SLOPE = 0.01
MASKED = -3.0e38


class Count:

    def __init__(self, sem, credit=0):
        self.sem, self.credit = sem, credit

    def done(self, n):
        return n + self.credit

    def room(self, i):
        return i + 1


class Chain:

    def __init__(self, eng, sem, steps, i, taken=0):
        self.eng, self.sem, self.base, self.steps, self.n = eng, sem, i * steps, steps, taken

    def link(self, ins):
        self.n += 1
        assert self.n <= self.steps
        ins.then_inc(self.sem, 1)
        self.eng.wait_ge(self.sem, self.base + self.n)


def pipeline(eng, tiles, stages, apart=0, tail=None, left=(), extra=()):
    end = tiles - apart
    deep = max(lag for _, lag in stages)

    def step(s, parity, lo, hi):
        for stage, lag in stages:
            if lo - lag >= 0 and hi - lag < tiles:
                stage(s - lag, (parity - lag) % 2)

    first = deep + (end - deep) % 2
    for s in range(first):
        step(s, s % 2, s, s)
    with eng.Fori(0, (end - first) // 2) as turn:
        for d in range(2):
            step(turn * 2 + (first + d), (first + d) % 2, first, end - 1)
    if tail is None:
        for s in range(end, tiles + deep):
            step(s, s % 2, s, s)
    else:
        due = {(stage, i) for stage, lag in stages for i in range(end - lag, tiles)}
        assert due == (set(tail) | set(left)) - set(extra)
        for stage, i in tail:
            stage(i, i % 2)


def after_first(stage):
    def rest(i, p):
        if not (isinstance(i, int) and i == 0):
            stage(i, p)
    return rest


def gnn_stack(nc, x, adj, w0, w_sa, a_sa, w_gcn, b_gcn, wa, ba, wb, bb, w2, b2, w3, out):
    N, D = x.shape
    T = -(-N // P)
    FULL = N // P
    TAIL = N - FULL * P
    NP = T * P
    KD = D // P
    assert D == 2 * P and T - FULL == 1 and w3.shape[0] == 2
    CH = [(c, min(c + BANK, N)) for c in range(0, N, BANK)]
    EB = BANK // P

    def kk(k):
        return P if k < FULL else TAIL

    ctx = ExitStack()
    with ctx:
        ctx.enter_context(nc.allow_non_contiguous_dma(reason="weight vectors as columns"))

        def sb(name, shape, dt=F32):
            return ctx.enter_context(nc.sbuf_tensor(name, shape, dt))

        def sem(name, credit=0):
            s = Count(ctx.enter_context(nc.semaphore(name)), credit)
            counts.append(s)
            return s

        counts = []

        adjT = sb("adjT", [P, T, NP])
        x_all = sb("x_all", [P, T, D])
        feats = sb("feats", [P, T, 2, D + 2])
        xs = sb("xs", [P, 2, D])
        xTs = sb("xTs", [P, 2, KD, P])
        vbuf = sb("vbuf", [P, 2, D])
        M3 = sb("M3", [P, 2, KD, D])
        Qs = sb("Qs", [P, 2, KD, P])
        ident = sb("ident", [P, P])
        identb = sb("identb", [P, P], BF16)
        W1 = sb("W1", [P, KD, 2 * D])
        Wcol = sb("Wcol", [P, KD, 6])
        nwl = sb("nwl", [P, KD])
        WLb = sb("WLb", [P, KD, P])
        W2 = sb("W2", [P, KD, D])
        W3 = sb("W3", [P, 2, KD, 2 * D])
        b1b = sb("b1b", [P, D])
        b2b = sb("b2b", [P, D])
        babb = sb("babb", [P, 2])
        hbab = sb("hbab", [P, 2])
        hattn = sb("hattn", [P, T, 2])
        nsr = sb("nsr", [P, T, 1])
        nsl = sb("nsl", [P, NP])
        deg = sb("deg", [P, T])
        pad_deg = sb("pad_deg", [P, T])
        nhalf = sb("nhalf", [P, 1])
        stats = sb("stats", [P, 2, 6])
        mv = sb("mv", [P, 2, 2])
        veps = sb("veps", [P, 2, 1])
        rstd = sb("rstd", [P, 2, 1])
        att_in = sb("att_in", [P, 2, 2])
        att_t = sb("att_t", [P, 2, 2])
        att = sb("att", [P, 2, 2])
        den = sb("den", [P, 2, 1])
        rden = sb("rden", [P, 2, 1])
        idle = sb("idle", [P, 1])
        idle_pool = sb("idle_pool", [P, 1])
        negmax = sb("negmax", [P, 2, 1])
        esum = sb("esum", [P, 2, 1])

        SLOT = T * D * 4
        arena = sb("arena", [P, 7 * T * D])
        base = nc.sbuf_base - 7 * SLOT

        def at(name, slot, shape, dt=F32, skip=0):
            return nc.alloc_sbuf_tensor_at(name, shape, dt, offset=base + slot * SLOT + skip)

        adj_rows = at("adj_rows", 0, [P, 2, NP])
        HALF = SLOT // 2
        rest = at("rest", 1, [P, T, P])
        hi = at("hi", 2, [P, 2, T, P], BF16)
        mid = at("mid", 2, [P, 2, T, P], BF16, HALF)
        lo = at("lo", 3, [P, 2, T, P], BF16)
        xw = at("xw", 3, [P, T, D], BF16, HALF)
        adjTs = at("adjTs", 0, [P, 2, T, P])
        escore = at("escore", 1, [P, 2, T, P])
        eT = at("eT", 3, [P, 2, T, P])
        hid = at("hid", 4, [P, T, 3, D], BF16)
        maskT = at("maskT", 2, [P, 2, T, P], BF16)
        signs = at("signs", 2, [P, 2, N], BF16, HALF)
        probs = at("probs", 2, [P, 2, NP])
        probsT = at("probsT", 3, [P, 2, T, P])
        xT = [at("xT0", 0, [P, KD, NP]), at("xT1", 1, [P, KD, NP])]
        W3T = at("W3T", 6, [P, 2, KD, D])
        x1 = at("x1", 6, [P, T, D])
        w0n = at("w0n", 4, [P, KD, D])
        KB = 2 * KD * D
        w0s = at("w0s", 6, [P, KD, D], BF16)
        w0neg = at("w0neg", 6, [P, KD, D], BF16, 2 * KB)
        w0T = at("w0T", 6, [P, KD, D], BF16, KB)
        pos = at("pos", 5, [P, T, D], BF16)
        posT = at("posT", 5, [P, KD, NP], BF16, HALF)
        a_b = at("a_b", 6, [P, 2 * D], F32, 4 * KB)
        dots = at("dots", 6, [P, D], F32, 8 * KB)
        hidden = at("hidden", 6, [P, 2, D], F32, 4 * KB)
        h_rest = at("h_rest", 6, [P, 2, D], F32, 6 * KB)

        psum = ctx.enter_context(nc.psum_tensor("psum", [P, 8, BANK], F32))
        Wh = [feats[:, :, 0, 0:D], feats[:, :, 1, 0:D]]

        def bank(b, lo_=0, hi_=BANK):
            return psum[:, b, lo_:hi_]

        def bankb(b):
            return psum[:, b, :].bitcast(BF16)

        adj_in_tail = sem("adj_in_tail")
        adj_in = [sem("adj_in_even"), sem("adj_in_odd")]
        x_in, w0_in, w_in, a_in, col_in = sem("x_in"), sem("w0_in"), sem("w_in"), sem("a_in"), sem("col_in")
        late_in = sem("late_in")
        pads_zero = sem("pads_zero")
        out_done = [sem("out_done_even", 16), sem("out_done_odd", 16)]
        dve_setup, consts_ready = sem("dve_setup"), sem("consts_ready")
        ident_ready, w0_signed, w0T_ps, w0T_ready = sem("ident_ready"), sem("w0_signed"), sem("w0T_ps"), sem("w0T_ready")
        cols_ready = sem("cols_ready")
        pos_ready, pos_ps, posT_ready, xw_ps, xw_ready = (
            sem("pos_ready"), sem("pos_ps"), sem("posT_ready"), sem("xw_ps"), sem("xw_ready"))

        class Phase:

            def __init__(s, n):
                s.agg_done = sem(n + "_agg_done", 2)
                s.acc_read = sem(n + "_acc_read", 2)
                s.fin_chain = sem(n + "_fin_chain")
                s.var_ready = sem(n + "_var_ready")
                s.rstd_ready = sem(n + "_rstd_ready")
                s.xs_ready = sem(n + "_xs_ready")
                s.x_stored = sem(n + "_x_stored", 2)
                s.xs_turned = sem(n + "_xs_turned", 2)
                s.xT_ready = sem(n + "_xT_ready", 1)
                s.proj_done = sem(n + "_proj_done", 2)
                s.proj_ready = sem(n + "_proj_ready", 1)

        A, B, C, D1, D2 = (Phase(n) for n in ("binary", "attn", "mean", "gat1", "gat2"))
        BANKS_T = -(-T // EB)
        adjT_turned = sem("adjT_turned", 2 * BANKS_T)
        adjT_banks_read = sem("adjT_banks_read", BANKS_T)
        rest_ready, mid_ready, lo_ready = sem("rest_ready"), sem("mid_ready"), sem("lo_ready")
        bprep_adj, bprep_score, bprep_exp = sem("stationary_adj_ready"), sem("score_ready"), sem("exp_ready", 2)
        aggz_done, score_chain, pool_chain = sem("aggz_done", 2), sem("score_chain"), sem("pool_chain")
        att_in_ready, att_ready, gate_in_ready, gate_ready = (
            sem("att_in_ready"), sem("att_ready"), sem("gate_in_ready"), sem("gate_ready"))
        sign_ready, deg_ready = sem("sign_ready"), sem("deg_ready", 2)
        hid_chain = sem("hid_chain")
        mask_ready = sem("mean_mask_ready")

        hid_split, last_chain, hid_last = sem("hid_split", 2), sem("last_chain"), sem("hid_last")
        w3_turned, w3T_ready, m3_ps, m3_ready = sem("w3_turned"), sem("w3T_ready"), sem("m3_ps"), sem("m3_ready")

        class Gat:
            def __init__(s, n):
                s.q_done = sem(n + "_q_done")
                s.Qs_ready = sem(n + "_Qs_ready")
                s.scores_done = sem(n + "_scores_done", 2)
                s.max_ready = sem(n + "_max_ready", 1)
                s.probs_ready = sem(n + "_probs_ready", 1)
                s.turned = sem(n + "_turned", 2)
                s.probsT_ready = sem(n + "_probsT_ready", 1)
                s.last_bank = sem(n + "_last_bank")

        G = [Gat("g1"), Gat("g2")]

        block = ctx.enter_context(nc.Block())

        def credits(eng, *cs):
            for c in cs:
                eng.sem_inc(c.sem, c.credit)

        def parts(engine, c, i, p):
            whole, rest_h = hidden[:, p:p + 1, :], h_rest[:, p:p + 1, :]
            c.link(engine.tensor_copy(hid[:, bass.ds(i, 1), 0, :], whole))
            carry(engine)
            c.link(engine.tensor_tensor(rest_h, whole, hid[:, bass.ds(i, 1), 0, :], ALU.subtract))
            c.link(engine.tensor_copy(hid[:, bass.ds(i, 1), 1, :], rest_h))
            carry(engine)
            return engine.tensor_tensor(hid[:, bass.ds(i, 1), 2, :], rest_h, hid[:, bass.ds(i, 1), 1, :], ALU.subtract)

        def carry(engine):
            if engine is nc.gpsimd:
                nc.gpsimd.tensor_tensor(idle_pool[:, :], nhalf[:, :], nhalf[:, :], ALU.add)

        @block.sync
        def _(sp):
            def load_rows(i, p):
                sp.wait_ge(adjT_turned.sem, (i + 1) * BANKS_T)
                sp.dma_start(adj_rows[:, p, 0:N], adj[i * P:(i + 1) * P, :] if isinstance(i, int) else
                             adj[bass.ds(i * P, P), :]).then_inc(adj_in[p].sem, 16)

            load_rows(0, 0)
            sp.dma_start(x_all[:, 0:FULL, :], x[0:FULL * P, :].rearrange("(t p) d -> p t d", p=P)).then_inc(x_in.sem, 16)
            sp.wait_ge(pads_zero.sem, 1)
            sp.dma_start(x_all[0:64, FULL, :], x[FULL * P:FULL * P + 64, :]).then_inc(x_in.sem, 16)
            sp.dma_start(x_all[64:TAIL, FULL, :], x[FULL * P + 64:N, :]).then_inc(x_in.sem, 16)
            load_rows(1, 1)
            with sp.Fori(0, FULL // 2 - 1) as pair:
                load_rows(pair * 2 + 2, 0)
                load_rows(pair * 2 + 3, 1)
            sp.wait_ge(adjT_turned.sem, (FULL + 1) * BANKS_T)
            sp.dma_start(adj_rows[0:64, 0, 0:N], adj[FULL * P:FULL * P + 64, :]).then_inc(adj_in_tail.sem, 16)
            sp.dma_start(adj_rows[64:TAIL, 0, 0:N], adj[FULL * P + 64:N, :]).then_inc(adj_in_tail.sem, 16)

            def store(i, p):
                sp.wait_ge(D2.xs_ready.sem, D2.xs_ready.done(i + 1))
                sp.dma_start(out[bass.ds(i * P, P), :], xs[:, p, :]).then_inc(out_done[p].sem, 16)

            with sp.Fori(0, FULL // 2) as pair:
                store(pair * 2, 0)
                store(pair * 2 + 1, 1)
            sp.wait_ge(D2.xs_ready.sem, D2.xs_ready.done(T))
            sp.dma_start(out[FULL * P:N, :], xs[0:TAIL, 0, :]).then_inc(out_done[0].sem, 16)
            sp.wait_ge(out_done[0].sem, 16 * (T + 1) // 2 + out_done[0].credit)
            sp.wait_ge(out_done[1].sem, 16 * (T // 2) + out_done[1].credit)

        @block.gpsimd
        def _(pool):
            credits(pool, hid_split, A.x_stored, B.x_stored, C.x_stored, D1.x_stored)
            nc.gpsimd.memset(ident[:, :], 0.0).then_inc(pool_chain.sem, 1)
            nc.gpsimd.memset(identb[:, :], 0.0).then_inc(pool_chain.sem, 1)
            nc.gpsimd.memset(nhalf[:, :], -0.5).then_inc(consts_ready.sem, 1)
            pool.wait_ge(pool_chain.sem, 2)
            for m in (ident, identb):
                nc.gpsimd.affine_select(out=m[:, :], in_=m[:, :], compare_op=ALU.not_equal, fill=1.0, base=0,
                                        pattern=[[-1, P]], channel_multiplier=1).then_inc(ident_ready.sem, 1)
            pool.dma_start(a_b[:, :], a_sa.partition_broadcast(P).rearrange("p a d -> p (a d)")).then_inc(a_in.sem, 16)
            for n, w in enumerate((wa, wb)):
                for half in range(2):
                    for k in range(KD):
                        c = (half * KD + k) * P
                        pool.dma_start(Wcol[:, k, 2 * half + n:2 * half + n + 1],
                                       w[:, c:c + P].rearrange("a p -> p a")).then_inc(col_in.sem, 16)
            pool.dma_start(babb[:, 0:1], ba.partition_broadcast(P)).then_inc(col_in.sem, 16)
            pool.dma_start(babb[:, 1:2], bb.partition_broadcast(P)).then_inc(col_in.sem, 16)
            pool.dma_start(b1b[:, :], b_gcn.partition_broadcast(P)).then_inc(late_in.sem, 16)
            pool.dma_start(b2b[:, :], b2.partition_broadcast(P)).then_inc(late_in.sem, 16)
            pool.dma_start(W2[:, :, :], w2.rearrange("(k p) n -> p k n", p=P)).then_inc(late_in.sem, 16)
            for l in range(2):
                pool.dma_start(W3[:, l, :, :], w3[l].rearrange("(k p) n -> p k n", p=P)).then_inc(late_in.sem, 16)
            pool.wait_ge(consts_ready.sem, 1)

            def rsqrt(ph):
                def stage(i, p):
                    pool.wait_ge(ph.var_ready.sem, ph.var_ready.done(i + 1))
                    nc.gpsimd.tensor_tensor(rstd[:, p, :], veps[:, p, :], nhalf[:, :], ALU.pow).then_inc(ph.rstd_ready.sem, 1)
                return stage

            def store_x(ph, dst):
                def stage(i, p):
                    pool.wait_ge(ph.xs_ready.sem, ph.xs_ready.done(i + 1))
                    nc.gpsimd.tensor_copy(dst[:, bass.ds(i, 1), :], xs[:, p:p + 1, :]).then_inc(ph.x_stored.sem, 1)
                return stage

            pipeline(pool, T, [(rsqrt(A), 2), (store_x(A, x_all), 2)])

            def split_hidden(i, p):
                if isinstance(i, int) and i == T - 1:
                    return
                pool.wait_ge(B.proj_ready.sem, B.proj_ready.done(i + 1))
                parts(nc.gpsimd, Chain(pool, hid_chain.sem, 3, i), i, p).then_inc(hid_split.sem, 1)

            pipeline(pool, T, [(rsqrt(B), 2), (store_x(B, x_all), 2), (split_hidden, 3)])
            pipeline(pool, T, [(rsqrt(C), 2), (store_x(C, x_all), 2)])
            pipeline(pool, T, [(store_x(D1, x1), 0)])
            pipeline(pool, T, [(rsqrt(D2), 0)])

        @block.scalar
        def _(act):
            credits(act, bprep_exp, deg_ready, A.xT_ready, B.xT_ready, C.xT_ready, D1.xT_ready, adjT_banks_read,
                    C.proj_ready, D1.proj_ready, G[0].probs_ready, G[1].probs_ready)
            act.dma_start(w0n[:, :, :], w0.rearrange("(k p) d -> p k d", p=P)).then_inc(w0_in.sem, 16)
            act.dma_start(W1[:, :, 0:D], w_gcn.rearrange("(k p) n -> p k n", p=P)).then_inc(w_in.sem, 16)
            act.dma_start(W1[:, :, D:2 * D], w_sa.rearrange("(k p) n -> p k n", p=P)).then_inc(w_in.sem, 16)

            def xT_evac(ph, b, whole=None):
                def stage(i, p):
                    act.wait_ge(ph.xs_turned.sem, ph.xs_turned.done(i + 1))
                    if whole is not None:
                        nc.scalar.activation(whole[:, :, bass.ds(i * P, P)], bank(b, 0, D).rearrange("p (k n) -> p k n", k=KD),
                                             ACT.Copy)
                    act.wait_ge(ph.proj_done.sem, ph.proj_done.room(i))
                    nc.scalar.activation(xTs[:, p, :, :], bank(b, 0, D).rearrange("p (k n) -> p k n", k=KD),
                                         ACT.Copy).then_inc(ph.xT_ready.sem, 1)
                return stage

            def adj_evac(i, p):
                act.wait_ge(A.agg_done.sem, A.agg_done.room(i))
                for g in range(BANKS_T):
                    k0, k1 = g * EB, min(g * EB + EB, T)
                    act.wait_ge(adjT_turned.sem, adjT_turned.done(i * BANKS_T + g + 1))
                    src = bank(g, 0, (k1 - k0) * P).rearrange("p (k n) -> p k n", n=P)
                    nc.scalar.activation(adjT[:, k0:k1, bass.ds(i * P, P)], src, ACT.Copy)
                    last = nc.scalar.activation(hi[:, p, k0:k1, :], src, ACT.Copy)
                    last.then_inc(adjT_banks_read.sem, 1)

            def middle_bits(i, p):
                act.wait_ge(rest_ready.sem, i + 1)
                act.wait_ge(A.agg_done.sem, A.agg_done.room(i))
                nc.scalar.activation(mid[:, p, :, :], rest[:, :, :], ACT.Copy).then_inc(mid_ready.sem, 1)

            adj_evac(0, 0)
            act.wait_ge(w0T_ps.sem, 1)
            nc.scalar.activation(w0T[:, :, :], bankb(7)[:, 0:KD * D].rearrange("p (k n) -> p k n", k=KD),
                                 ACT.Copy).then_inc(w0T_ready.sem, 1)
            middle_bits(0, 0)

            for g in range(BANKS_T):
                t0, t1 = g * EB, min(g * EB + EB, T)
                act.wait_ge(pos_ps.sem, g + 1)
                nc.scalar.activation(posT[:, :, t0 * P:t1 * P],
                                     bankb(5 + g).rearrange("p (k n) -> p k n", k=KD)[:, :, 0:(t1 - t0) * P],
                                     ACT.Copy).then_inc(posT_ready.sem, 1)

            def copy_adj(i, p):
                if isinstance(i, int) and i == 0:
                    act.wait_ge(adjT_turned.sem, adjT_turned.done(BANKS_T * T))
                act.wait_ge(aggz_done.sem, aggz_done.room(i))
                nc.scalar.activation(adjTs[:, p, :, :], adjT[:, :, bass.ds(i * P, P)], ACT.Copy).then_inc(bprep_adj.sem, 1)

            xT_a = xT_evac(A, 5)
            pipeline(act, T, [(xT_a, 3), (after_first(adj_evac), 0), (after_first(middle_bits), 0)],
                     tail=[(xT_a, T - 3), (xT_a, T - 2), (copy_adj, 0), (xT_a, T - 1)], extra=[(copy_adj, 0)])

            def exp_scores(i, p):
                act.wait_ge(bprep_score.sem, i + 1)
                act.wait_ge(B.agg_done.sem, B.agg_done.room(i))
                nc.scalar.activation(eT[:, p, :, :], escore[:, p, :, :], ACT.Exp).then_inc(bprep_exp.sem, 1)

            def gates(i, p):
                act.wait_ge(att_in_ready.sem, i + 1)
                nc.scalar.activation(att_t[:, p, :], att_in[:, p, :], ACT.Tanh).then_inc(att_ready.sem, 1)
                act.wait_ge(gate_in_ready.sem, i + 1)
                nc.scalar.activation(vbuf[:, p, :], vbuf[:, p, :], ACT.Tanh, scale=0.5).then_inc(gate_ready.sem, 1)

            def w3T_evac(l, _):
                if l == 1:
                    act.wait_ge(m3_ps.sem, 1)
                for half, b in ((0, 6), (1, 4)):
                    act.wait_ge(w3_turned.sem, 2 * l + half + 1)
                    nc.scalar.activation(W3T[:, half, :, :], bank(b).rearrange("p (k n) -> p k n", k=KD),
                                         ACT.Copy).then_inc(w3T_ready.sem, 1)

            def m3_evac(l, _):
                act.wait_ge(m3_ps.sem, l + 1)
                nc.scalar.activation(M3[:, l, :, :], bank(1).rearrange("p (k n) -> p k n", k=KD),
                                     ACT.Copy).then_inc(m3_ready.sem, 1)

            xT_b = xT_evac(B, 5)
            pipeline(act, T, [(after_first(copy_adj), 0), (gates, 2), (xT_b, 3), (exp_scores, 0)],
                     tail=[(xT_b, T - 3), (gates, T - 2), (xT_b, T - 2), (w3T_evac, 0), (gates, T - 1), (m3_evac, 0),
                           (w3T_evac, 1), (xT_b, T - 1), (m3_evac, 1)],
                     extra=[(w3T_evac, 0), (w3T_evac, 1), (m3_evac, 0), (m3_evac, 1)])

            def proj_evac(ph, wh):
                def stage(i, p):
                    act.wait_ge(ph.proj_done.sem, ph.proj_done.done(i + 1))
                    nc.scalar.activation(wh[:, bass.ds(i, 1), :], bank(7, 0, D).unsqueeze(1), ACT.Copy).then_inc(ph.proj_ready.sem, 1)
                return stage

            class q_evac:

                def __init__(self, g):
                    self.g = g

                def evac(self, i, p, b):
                    act.wait_ge(self.g.q_done.sem, i + 1)
                    act.wait_ge(self.g.scores_done.sem, self.g.scores_done.room(i))
                    nc.scalar.activation(Qs[:, p, :, :], bank(b, 0, D).rearrange("p (m n) -> p m n", m=KD),
                                         ACT.Copy).then_inc(self.g.Qs_ready.sem, 1)

                def start(self, i, p):
                    self.evac(0, 0, 2)

                def __call__(self, i, p):
                    if not (isinstance(i, int) and i == 0):
                        self.evac(i, p, 7)

            def degree(i, p):
                act.wait_ge(deg_ready.sem, deg_ready.room(i))
                nc.scalar.activation(signs[:, p:p + 1, :], adjT[:, bass.ds(i, 1), 0:N], ACT.Sign).then_inc(sign_ready.sem, 1)
                act.wait_ge(sign_ready.sem, i + 1)
                nc.scalar.activation(signs[:, p:p + 1, :], signs[:, p:p + 1, :], ACT.Square,
                                     accum_out=deg[:, bass.ds(i, 1)]).then_inc(deg_ready.sem, 1)

            xT_c, proj_c, q_1, q_2 = xT_evac(C, 5, xT[0]), proj_evac(C, Wh[0]), q_evac(G[0]), q_evac(G[1])
            pipeline(act, T, [(xT_c, 3), (proj_c, 3), (degree, 0)],
                     tail=[(xT_c, T - 3), (proj_c, T - 3), (xT_c, T - 2), (q_1.start, 0), (xT_c, T - 1), (proj_c, T - 2),
                           (proj_c, T - 1)], extra=[(q_1.start, 0)])

            def exp_row(g):
                def stage(i, p):
                    act.wait_ge(g.max_ready.sem, g.max_ready.done(i + 1))
                    act.wait_ge(g.turned.sem, g.turned.room(i))
                    nc.scalar.activation(probs[:, p, 0:N], psum[:, 0:len(CH), :].rearrange("p b n -> p (b n)")[:, 0:N],
                                         ACT.Exp, bias=negmax[:, p, :], accum_out=esum[:, p, :]).then_inc(g.probs_ready.sem, 1)
                return stage

            xT_d, proj_d = xT_evac(D1, 7, xT[1]), proj_evac(D1, Wh[1])
            pipeline(act, T, [(q_1, 0), (xT_d, 3), (proj_d, 3), (exp_row(G[0]), 0)],
                     tail=[(xT_d, T - 3), (q_2.start, 0), (proj_d, T - 3), (xT_d, T - 2), (proj_d, T - 2), (xT_d, T - 1),
                           (proj_d, T - 1)], extra=[(q_2.start, 0)])
            pipeline(act, T, [(q_2, 0), (exp_row(G[1]), 0)])

        @block.vector
        def _(dve):
            credits(dve, A.acc_read, B.acc_read, C.acc_read, D1.acc_read, D2.acc_read,
                    A.proj_ready, B.proj_ready, G[0].max_ready, G[1].max_ready, G[0].probsT_ready, G[1].probsT_ready)
            for o in out_done:
                dve.sem_inc(o.sem, o.credit)
            nc.vector.memset(x_all[:, FULL, :], 0.0).then_inc(dve_setup.sem, 1)
            dve.wait_ge(dve_setup.sem, 1)
            nc.vector.memset(adj_rows[:, :, N:NP], 0.0).then_inc(pads_zero.sem, 1)
            nc.vector.memset(feats[:, :, 1, D:D + 2], 1.0)
            nc.vector.memset(WLb[:, :, :], 0.0).then_inc(dve_setup.sem, 1)
            nc.vector.memset(pad_deg[:, :], 0.0).then_inc(dve_setup.sem, 1)
            dve.wait_ge(dve_setup.sem, 3)
            nc.vector.memset(pad_deg[:, FULL:T], 1.0).then_inc(dve_setup.sem, 1)
            dve.wait_ge(dve_setup.sem, 4)
            nc.vector.memset(pad_deg[0:TAIL, FULL:T], 0.0).then_inc(dve_setup.sem, 1)
            dve.wait_ge(w0_in.sem, 16)
            nc.vector.tensor_scalar(w0neg[:, :, :], w0n[:, :, :], 0.0, None, ALU.is_lt).then_inc(dve_setup.sem, 1)
            dve.wait_ge(dve_setup.sem, 6)
            nc.vector.scalar_tensor_tensor(out=w0s[:, :, :], in0=w0n[:, :, :], scalar=0.0, in1=w0neg[:, :, :],
                                           op0=ALU.is_gt, op1=ALU.subtract).then_inc(w0_signed.sem, 1)
            def rest_bits(i, p):
                if isinstance(i, int) and i == 0:
                    pass
                else:
                    dve.wait_ge(lo_ready.sem, i)
                for g in range(BANKS_T):
                    k0, k1 = g * EB, min(g * EB + EB, T)
                    dve.wait_ge(adjT_banks_read.sem, adjT_banks_read.done(BANKS_T * i + g + 1))
                    last = nc.vector.tensor_tensor(rest[:, k0:k1, :], adjT[:, k0:k1, bass.ds(i * P, P)], hi[:, p, k0:k1, :],
                                                   ALU.subtract)
                last.then_inc(rest_ready.sem, 1)

            def lower_bits(i, p):
                dve.wait_ge(mid_ready.sem, i + 1)
                nc.vector.tensor_tensor(lo[:, p, :, :], rest[:, :, :], mid[:, p, :, :], ALU.subtract).then_inc(lo_ready.sem, 1)

            rest_bits(0, 0)
            dve.wait_ge(x_in.sem, 48)
            for t0 in range(0, T, EB):
                t1 = min(t0 + EB, T)
                nc.vector.tensor_scalar(pos[:, t0:t1, :], x_all[:, t0:t1, :], 0.0, None, ALU.is_gt).then_inc(pos_ready.sem, 1)
            lower_bits(0, 0)
            dve.wait_ge(a_in.sem, 16)
            dve.wait_ge(w_in.sem, 16 * 2)
            for half in range(2):
                for k in range(KD):
                    acc = nwl[:, k:k + 1] if half == 0 else Wcol[:, k, 4:5]
                    nc.vector.tensor_tensor_reduce(out=dots[:, :], in0=W1[:, k, D:2 * D],
                                                   in1=a_b[:, half * D:(half + 1) * D], scale=-1.0, scalar=0.0,
                                                   op0=ALU.mult, op1=ALU.add, accum_out=acc).then_inc(dve_setup.sem, 1)
                    dve.wait_ge(dve_setup.sem, 7 + half * KD + k)
            for k in range(KD):
                nc.vector.tensor_scalar(WLb[:, k, :], WLb[:, k, :], nwl[:, k:k + 1], None, ALU.add)
            for t0 in range(0, T, 2):
                t1 = min(t0 + 2, T)
                dve.wait_ge(xw_ps.sem, t0 // 2 + 1)
                nc.vector.tensor_copy(xw[:, t0:t1, :], bank(t0 // 2, 0, (t1 - t0) * D).rearrange("p (t n) -> p t n", n=D))\
                    .then_inc(xw_ready.sem, 1)

            dve.wait_ge(col_in.sem, 16 * 10)
            nc.vector.tensor_scalar(hbab[:, :], babb[:, :], 0.5, None, ALU.mult).then_inc(cols_ready.sem, 1)
            dve.wait_ge(cols_ready.sem, 1)

            def norm_stats(ph, i, p, c):
                c.link(nc.vector.bn_stats(stats[:, p, :], vbuf[:, p, :]))
                nc.vector.memset(idle[:, :], 0.0)
                c.link(nc.vector.bn_aggr(mv[:, p, :], stats[:, p, :]))
                nc.vector.tensor_scalar(veps[:, p, :], mv[:, p, 1:2], LN_EPS, None, ALU.add).then_inc(ph.var_ready.sem, 1)

            def norm_apply(ph, free):
                def stage(i, p):
                    free(i, p)
                    dve.wait_ge(ph.rstd_ready.sem, i + 1)
                    nc.vector.tensor_scalar(xs[:, p, :], vbuf[:, p, :], mv[:, p, 0:1], rstd[:, p, :], ALU.subtract,
                                            ALU.mult).then_inc(ph.xs_ready.sem, 1)
                return stage

            def xs_free(ph):
                def free(i, p):
                    dve.wait_ge(ph.xs_turned.sem, ph.xs_turned.room(i))
                    dve.wait_ge(ph.x_stored.sem, ph.x_stored.room(i))
                return free

            def finish_a(i, p):
                c = Chain(dve, A.fin_chain.sem, 3, i)
                dve.wait_ge(A.agg_done.sem, A.agg_done.done(i + 1))
                ins = nc.vector.scalar_tensor_tensor(out=vbuf[:, p:p + 1, :], in0=bank(3 + p, 0, D).unsqueeze(1), scalar=0.0,
                                                     in1=x_all[:, bass.ds(i, 1), :], op0=ALU.max, op1=ALU.add)
                c.link(ins)
                norm_stats(A, i, p, c)

            def evac_a(i, p):
                dve.wait_ge(A.proj_done.sem, A.proj_done.done(i + 1))
                nc.vector.tensor_copy(feats[:, bass.ds(i, 1), :, 0:D],
                                      bank(7).rearrange("p (a b n) -> p a b n", a=1, b=2))
                nc.vector.tensor_copy(feats[:, bass.ds(i, 1), 0:1, D:D + 2], bank(6, 0, 2).unsqueeze(1).unsqueeze(1))
                nc.vector.scalar_tensor_tensor(out=hattn[:, bass.ds(i, 1), :], in0=bank(6, 2, 4).unsqueeze(1), scalar=0.5,
                                               in1=hbab[:, :].unsqueeze(1), op0=ALU.mult, op1=ALU.add)
                nc.vector.tensor_copy(nsr[:, bass.ds(i, 1), :], bank(6, 4, 5).unsqueeze(1))
                nc.vector.tensor_copy(nsl[:, bass.ds(i * P, P)], bank(6, P, 2 * P)).then_inc(A.proj_ready.sem, 1)

            def mask_b(i, p):
                dve.wait_ge(bprep_exp.sem, bprep_exp.room(i))
                nc.vector.tensor_scalar(escore[:, p, :, :], adjT[:, :, bass.ds(i * P, P)], 0.0, MASKED, ALU.is_equal,
                                        ALU.mult).then_inc(score_chain.sem, 1)

            def add_scores(i, p, ks):
                for k in ks:
                    last = nc.vector.scalar_tensor_tensor(out=escore[:, p, k, :], in0=escore[:, p, k, :], scalar=nsr[:, k, :],
                                                          in1=nsl[:, bass.ds(i * P, P)], op0=ALU.add, op1=ALU.add)
                return last

            EARLY = T - 4

            def first_scores(k0, _):
                if k0 == 0:
                    dve.wait_ge(A.proj_ready.sem, A.proj_ready.done(T - 2))
                    dve.wait_ge(score_chain.sem, 1)
                add_scores(0, 0, range(4) if k0 == 0 else range(4, EARLY))

            apply_a = norm_apply(A, xs_free(A))
            pipeline(dve, T, [(finish_a, 2), (after_first(rest_bits), 0), (apply_a, 2), (evac_a, 3), (after_first(lower_bits), 0)],
                     tail=[(finish_a, T - 2), (apply_a, T - 2), (evac_a, T - 3), (mask_b, 0), (first_scores, 0),
                           (finish_a, T - 1), (apply_a, T - 1), (first_scores, 4), (evac_a, T - 2)],
                     extra=[(mask_b, 0), (first_scores, 0), (first_scores, 4)],
                     left=[(evac_a, T - 1)])

            def scores_b(i, p):
                dve.wait_ge(score_chain.sem, i * 2 + 1)
                if isinstance(i, int) and i == 0:
                    dve.wait_ge(A.proj_ready.sem, A.proj_ready.done(FULL))
                    add_scores(i, p, range(EARLY, FULL))
                    evac_a(T - 1, (T - 1) % 2)
                    dve.wait_ge(A.proj_ready.sem, A.proj_ready.done(T))
                    last = add_scores(i, p, [FULL])
                else:
                    last = add_scores(i, p, range(T))
                Chain(dve, score_chain.sem, 2, i, 1).link(last)
                nc.vector.scalar_tensor_tensor(out=escore[:, p, :, :], in0=escore[:, p, :, :], scalar=SLOPE,
                                               in1=escore[:, p, :, :], op0=ALU.mult, op1=ALU.min).then_inc(bprep_score.sem, 1)

            def finish_b(i, p):
                c = Chain(dve, B.fin_chain.sem, 10, i)
                dve.wait_ge(aggz_done.sem, aggz_done.done(i + 1))
                nc.vector.scalar_tensor_tensor(out=att_in[:, p:p + 1, :], in0=bank(p, D, D + 2).unsqueeze(1), scalar=0.5,
                                               in1=hattn[:, bass.ds(i, 1), :], op0=ALU.mult, op1=ALU.add).then_inc(att_in_ready.sem, 1)
                c.link(nc.vector.tensor_tensor(vbuf[:, p, :], bank(p, 0, D), b1b[:, :], ALU.add))
                dve.wait_ge(B.agg_done.sem, B.agg_done.done(i + 1))
                c.link(nc.vector.tensor_scalar(den[:, p, :], bank(2 + p, D, D + 1), ATTN_EPS, None, ALU.add))
                c.link(nc.vector.reciprocal(rden[:, p, :], den[:, p, :]))
                dve.wait_ge(att_ready.sem, i + 1)
                c.link(nc.vector.tensor_scalar(att[:, p, :], att_t[:, p, :], 0.5, 0.5, ALU.mult, ALU.add))
                c.link(nc.vector.tensor_scalar(vbuf[:, p, :], vbuf[:, p, :], att[:, p, 1:2], None, ALU.mult))
                c.link(nc.vector.tensor_tensor(rden[:, p, :], rden[:, p, :], att[:, p, 0:1], ALU.mult))
                nc.vector.scalar_tensor_tensor(out=vbuf[:, p, :], in0=bank(2 + p, 0, D), scalar=rden[:, p, :], in1=vbuf[:, p, :],
                                               op0=ALU.mult, op1=ALU.add).then_inc(gate_in_ready.sem, 1)

            def finish_b2(i, p):
                c = Chain(dve, B.fin_chain.sem, 10, i, 6)
                dve.wait_ge(gate_ready.sem, i + 1)
                c.link(nc.vector.tensor_scalar(vbuf[:, p, :], vbuf[:, p, :], 0.5, 0.5, ALU.mult, ALU.add))
                c.link(nc.vector.tensor_tensor(vbuf[:, p:p + 1, :], vbuf[:, p:p + 1, :], x_all[:, bass.ds(i, 1), :], ALU.add))
                norm_stats(B, i, p, c)

            def evac_b(i, p):
                dve.wait_ge(hid_split.sem, hid_split.room(i))
                dve.wait_ge(B.proj_done.sem, B.proj_done.done(i + 1))
                nc.vector.tensor_tensor(hidden[:, p, :], bank(7, 0, D), b2b[:, :], ALU.add).then_inc(B.proj_ready.sem, 1)
                if isinstance(i, int) and i == T - 1:
                    dve.wait_ge(B.proj_ready.sem, B.proj_ready.done(T))
                    parts(nc.vector, Chain(dve, last_chain.sem, 3, 0), i, p).then_inc(hid_last.sem, 1)

            def mask_tile(i, p):
                nc.vector.tensor_scalar(maskT[:, p, :, :], adjT[:, :, bass.ds(i * P, P)], 0.0, None,
                                        ALU.not_equal).then_inc(mask_ready.sem, 1)

            def mask(i, p):
                if isinstance(i, int) and i == 0:
                    return
                dve.wait_ge(C.agg_done.sem, C.agg_done.room(i))
                mask_tile(i, p)

            dve.wait_ge(late_in.sem, 16 * 5)
            apply_b = norm_apply(B, xs_free(B))
            pipeline(dve, T, [(finish_b, 3), (scores_b, 1), (finish_b2, 3), (evac_b, 4), (after_first(mask_b), 0), (apply_b, 3)],
                     tail=[(finish_b, T - 3), (scores_b, T - 1), (finish_b2, T - 3), (evac_b, T - 4), (apply_b, T - 3),
                           (finish_b, T - 2), (finish_b2, T - 2), (apply_b, T - 2), (evac_b, T - 3), (mask_tile, 0), (evac_b, T - 2),
                           (finish_b, T - 1), (finish_b2, T - 1), (apply_b, T - 1), (evac_b, T - 1)], extra=[(mask_tile, 0)])

            def finish_c(i, p):
                c = Chain(dve, C.fin_chain.sem, 5, i)
                r = rden[:, p, :]
                dve.wait_ge(deg_ready.sem, deg_ready.done(i + 1))
                c.link(nc.vector.tensor_tensor(r, deg[:, bass.ds(i, 1)], pad_deg[:, bass.ds(i, 1)], ALU.add))
                c.link(nc.vector.reciprocal(r, r))
                dve.wait_ge(C.agg_done.sem, C.agg_done.done(i + 1))
                c.link(nc.vector.scalar_tensor_tensor(out=vbuf[:, p:p + 1, :], in0=bank(3 + p, 0, D).unsqueeze(1), scalar=r,
                                                      in1=x_all[:, bass.ds(i, 1), :], op0=ALU.mult, op1=ALU.add))
                norm_stats(C, i, p, c)

            apply_c = norm_apply(C, xs_free(C))
            pipeline(dve, T, [(finish_c, 2), (mask, 0), (apply_c, 2)])

            nc.vector.memset(probs[:, :, N:NP], 0.0).then_inc(pads_zero.sem, 1)

            def turn_evac(g):
                def stage(i, p):
                    dve.wait_ge(g.turned.sem, g.turned.done(i + 1))
                    if isinstance(i, int) and i == T - 1:
                        for b in range(BANKS_T):
                            k0, k1 = b * EB, min(b * EB + EB, T)
                            nc.vector.tensor_tensor(probsT[:, p, k0:k1, :], bank(3 + b, 0, (k1 - k0) * P).rearrange("p (k n) -> p k n", n=P),
                                                    adjT[:, k0:k1, bass.ds(i * P, P)], ALU.mult).then_inc(g.last_bank.sem, 1)
                        return
                    nc.vector.tensor_tensor(probsT[:, p, :, :], psum[:, 3:3 + BANKS_T, :].rearrange("p b (k n) -> p (b k) n", n=P)[:, 0:T, :],
                                            adjT[:, :, bass.ds(i * P, P)], ALU.mult).then_inc(g.probsT_ready.sem, 1)
                return stage

            def row_max(g):
                def stage(i, p):
                    dve.wait_ge(g.scores_done.sem, g.scores_done.done(i + 1))
                    nc.vector.tensor_reduce(negmax[:, p, :], psum[:, 0:len(CH), :].rearrange("p b n -> p (b n)")[:, 0:N], AX.X,
                                            ALU.max, negate=True).then_inc(g.max_ready.sem, 1)
                return stage

            def gat_out(ph, c, i, p, xin):
                dve.wait_ge(ph.agg_done.sem, ph.agg_done.done(i + 1))
                c.link(nc.vector.reciprocal(rden[:, p, :], esum[:, p, :]))
                ins = nc.vector.scalar_tensor_tensor(out=vbuf[:, p:p + 1, :], in0=bank(6, 0, D).unsqueeze(1), scalar=rden[:, p, :],
                                                     in1=xin[:, bass.ds(i, 1), :], op0=ALU.mult, op1=ALU.add)
                ins.then_inc(ph.acc_read.sem, 1)

            def out_d1(i, p):
                gat_out(D1, Chain(dve, D1.fin_chain.sem, 1, i), i, p, x_all)

            def finish_d1(i, p):
                dve.wait_ge(D1.acc_read.sem, D1.acc_read.done(i + 1))
                xs_free(D1)(i, p)
                nc.vector.scalar_tensor_tensor(out=xs[:, p, :], in0=vbuf[:, p, :], scalar=SLOPE, in1=vbuf[:, p, :],
                                               op0=ALU.mult, op1=ALU.max).then_inc(D1.xs_ready.sem, 1)

            dve.wait_ge(C.x_stored.sem, C.x_stored.done(T))
            turn_1, turn_2 = turn_evac(G[0]), turn_evac(G[1])
            pipeline(dve, T, [(turn_1, 1), (out_d1, 2), (finish_d1, 2), (row_max(G[0]), 0)],
                     tail=[(out_d1, T - 2), (turn_1, T - 1), (finish_d1, T - 2), (out_d1, T - 1), (finish_d1, T - 1)])

            def out_free(i, p):
                dve.wait_ge(out_done[p].sem, (i - p) * 8 + 16)

            def out_d2(i, p):
                gat_out(D2, Chain(dve, D2.fin_chain.sem, 5, i), i, p, x1)

            def finish_d2(i, p):
                c = Chain(dve, D2.fin_chain.sem, 5, i, 1)
                dve.wait_ge(D2.acc_read.sem, D2.acc_read.done(i + 1))
                c.link(nc.vector.scalar_tensor_tensor(out=vbuf[:, p, :], in0=vbuf[:, p, :], scalar=SLOPE, in1=vbuf[:, p, :],
                                                      op0=ALU.mult, op1=ALU.max))
                c.link(nc.vector.tensor_tensor(vbuf[:, p:p + 1, :], vbuf[:, p:p + 1, :], x_all[:, bass.ds(i, 1), :], ALU.add))
                norm_stats(D2, i, p, c)

            apply_d = norm_apply(D2, out_free)
            dve.wait_ge(D1.x_stored.sem, D1.x_stored.done(T))
            pipeline(dve, T, [(turn_2, 1), (out_d2, 2), (finish_d2, 2), (apply_d, 2), (row_max(G[1]), 0)],
                     tail=[(out_d2, T - 2), (turn_2, T - 1), (finish_d2, T - 2), (apply_d, T - 2), (out_d2, T - 1),
                           (finish_d2, T - 1), (apply_d, T - 1)])

        @block.tensor
        def _(pe):
            credits(pe, adjT_turned, aggz_done)
            for ph in (A, B, C, D1, D2):
                credits(pe, ph.agg_done, ph.xs_turned, ph.proj_done)
            for g in G:
                credits(pe, g.scores_done, g.turned)
            pe.wait_ge(ident_ready.sem, 2)

            def adj_turn(i, p):
                if isinstance(i, int) and i == FULL:
                    pe.wait_ge(adj_in_tail.sem, 32)
                else:
                    pe.wait_ge(adj_in[p].sem, (i - p) * 8 + 16)
                for g in range(BANKS_T):
                    pe.wait_ge(adjT_banks_read.sem, i * BANKS_T + g + 1)
                    for k in range(g * EB, min(g * EB + EB, T)):
                        last = nc.tensor.transpose(bank(g, (k % EB) * P, (k % EB) * P + P), adj_rows[:, p, k * P:(k + 1) * P],
                                                   ident[:, :])
                    last.then_inc(adjT_turned.sem, 1)

            pe.wait_ge(pads_zero.sem, 1)
            adj_turn(0, 0)
            pe.wait_ge(w0_signed.sem, 1)
            w0T_v = bankb(7)[:, 0:KD * D].rearrange("p (k n) -> p k n", k=KD)
            for o in range(KD):
                for k in range(KD):
                    last = nc.tensor.transpose(w0T_v[:, k, o * P:(o + 1) * P], w0s[:, o, k * P:(k + 1) * P], identb[:, :])
            last.then_inc(w0T_ps.sem, 1)

            pe.wait_ge(w0T_ready.sem, 1)
            for g in range(BANKS_T):
                t0, t1 = g * EB, min(g * EB + EB, T)
                pe.wait_ge(pos_ready.sem, g + 1)
                for t in range(t0, t1):
                    for k in range(KD):
                        c = k * EB * P + (t - t0) * P
                        last = nc.tensor.transpose(bankb(5 + g)[:, c:c + P], pos[:, t, k * P:(k + 1) * P], identb[:, :])
                last.then_inc(pos_ps.sem, 1)
            pe.wait_ge(adjT_banks_read.sem, adjT_banks_read.done(BANKS_T))
            for t in range(T):
                if t % EB == 0:
                    pe.wait_ge(posT_ready.sem, t // EB + 1)
                for k in range(KD):
                    last = nc.tensor.matmul(bank(t // 2, (t % 2) * D, (t % 2 + 1) * D), posT[:, k, t * P:(t + 1) * P], w0T[:, k, :],
                                            start=(k == 0), stop=(k == KD - 1))
                if t % 2 or t == T - 1:
                    last.then_inc(xw_ps.sem, 1)
            pe.wait_ge(xw_ready.sem, BANKS_T)

            def turn_x(ph, b, bank_free=None):
                def stage(i, p):
                    pe.wait_ge(ph.xs_ready.sem, i + 1)
                    if bank_free is None:
                        pe.wait_ge(ph.xT_ready.sem, ph.xT_ready.room(i))
                    else:
                        bank_free(i)
                    for k in range(KD):
                        last = nc.tensor.transpose(bank(b, k * P, (k + 1) * P), xs[:, p, k * P:(k + 1) * P], ident[:, :])
                    last.then_inc(ph.xs_turned.sem, 1)
                return stage

            def agg_a(i, p):
                pe.wait_ge(lo_ready.sem, i + 1)
                if isinstance(i, int) and i == 0:
                    pe.wait_ge(xw_ready.sem, -(-T // 2))
                if not (isinstance(i, int) and i < 2):
                    pe.wait_ge(A.xs_ready.sem, i - 1)
                for k in range(T):
                    for part in (hi, mid, lo):
                        last = nc.tensor.matmul(bank(3 + p, 0, D), part[0:kk(k), p, k, :], xw[0:kk(k), k, :],
                                                start=(k == 0 and part is hi), stop=(k == T - 1 and part is lo))
                last.then_inc(A.agg_done.sem, 1)

            def proj_a(i, p):
                if isinstance(i, int) and i == 0:
                    pe.wait_ge(cols_ready.sem, 1)
                pe.wait_ge(A.xT_ready.sem, A.xT_ready.done(i + 1))
                pe.wait_ge(A.proj_ready.sem, A.proj_ready.room(i))
                for k in range(KD):
                    nc.tensor.matmul(bank(7), xTs[:, p, k, :], W1[:, k, :], start=(k == 0), stop=(k == KD - 1))
                for k in range(KD):
                    nc.tensor.matmul(bank(6, 0, 5), xTs[:, p, k, :], Wcol[:, k, 0:5], start=(k == 0), stop=(k == KD - 1))
                for k in range(KD):
                    last = nc.tensor.matmul(bank(6, P, 2 * P), WLb[:, k, :], xTs[:, p, k, :], start=(k == 0), stop=(k == KD - 1))
                last.then_inc(A.proj_done.sem, 1)

            pipeline(pe, T, [(turn_x(A, 5), 3), (after_first(adj_turn), 0), (proj_a, 3), (agg_a, 1)], apart=1)

            def agg_z(i, p):
                if isinstance(i, int) and i == 0:
                    pe.wait_ge(A.proj_ready.sem, A.proj_ready.done(FULL))
                pe.wait_ge(bprep_adj.sem, i + 1)
                if not (isinstance(i, int) and i < 2):
                    pe.wait_ge(gate_in_ready.sem, i - 1)
                for k in range(T):
                    if k == FULL and isinstance(i, int) and i == 0:
                        pe.wait_ge(A.proj_ready.sem, A.proj_ready.done(T))
                    last = nc.tensor.matmul(bank(p, 0, D + 2), adjTs[0:kk(k), p, k, :], feats[0:kk(k), k, 0, :],
                                            start=(k == 0), stop=(k == T - 1))
                last.then_inc(aggz_done.sem, 1)

            def agg_h(i, p):
                pe.wait_ge(bprep_exp.sem, bprep_exp.done(i + 1))
                for k in range(T):
                    last = nc.tensor.matmul(bank(2 + p, 0, D + 1), eT[0:kk(k), p, k, :], feats[0:kk(k), k, 1, 0:D + 1],
                                            start=(k == 0), stop=(k == T - 1))
                last.then_inc(B.agg_done.sem, 1)

            def proj_b(i, p):
                pe.wait_ge(B.xT_ready.sem, B.xT_ready.done(i + 1))
                pe.wait_ge(B.proj_ready.sem, B.proj_ready.room(i))
                for k in range(KD):
                    last = nc.tensor.matmul(bank(7, 0, D), xTs[:, p, k, :], W2[:, k, :], start=(k == 0), stop=(k == KD - 1))
                last.then_inc(B.proj_done.sem, 1)

            def agg_c(i, p, ks=None):
                first_tile = isinstance(i, int) and i == 0
                pe.wait_ge(mask_ready.sem, i + 1)
                if not (isinstance(i, int) and i < 2):
                    pe.wait_ge(C.xs_ready.sem, i - 1)
                if first_tile and ks is None:
                    ks = range(T - 3, T)
                for k in range(T) if ks is None else ks:
                    if first_tile:
                        if k < T - 1:
                            pe.wait_ge(hid_split.sem, hid_split.done(k + 1))
                        else:
                            pe.wait_ge(hid_last.sem, 1)
                    for part in range(3):
                        last = nc.tensor.matmul(bank(3 + p, 0, D), maskT[0:kk(k), p, k, :], hid[0:kk(k), k, part, :],
                                                start=(k == 0 and part == 0), stop=(k == T - 1 and part == 2))
                if k == T - 1:
                    last.then_inc(C.agg_done.sem, 1)

            turn_b = turn_x(B, 5)

            def turn_w3(l, _):
                if l == 0:
                    pe.wait_ge(late_in.sem, 16 * 5)
                pe.wait_ge(A.proj_ready.sem, A.proj_ready.done(T))
                for half, b in ((0, 6), (1, 4)):
                    if l == 1:
                        pe.wait_ge(w3T_ready.sem, half + 1)
                    for e in range(KD):
                        for k in range(KD):
                            last = nc.tensor.transpose(bank(b, e * D + k * P, e * D + (k + 1) * P),
                                                       W3[:, l, k, half * D + e * P:half * D + (e + 1) * P], ident[:, :])
                    last.then_inc(w3_turned.sem, 1)

            def mul_w3(l, _):
                pe.wait_ge(w3T_ready.sem, 2 * l + 2)
                if l == 1:
                    pe.wait_ge(m3_ready.sem, 1)
                for m in range(KD):
                    for e in range(KD):
                        last = nc.tensor.matmul(bank(1, m * D, (m + 1) * D), W3T[:, 0, e, m * P:(m + 1) * P], W3T[:, 1, e, :],
                                                start=(e == 0), stop=(e == KD - 1))
                last.then_inc(m3_ps.sem, 1)

            def agg_c_start(i, p):
                agg_c(0, 0, range(T - 3))

            pipeline(pe, T, [(agg_z, 1), (turn_b, 3), (agg_h, 1), (proj_b, 3)],
                     tail=[(turn_b, T - 3), (agg_z, T - 1), (proj_b, T - 3), (agg_h, T - 1), (turn_b, T - 2), (turn_w3, 0),
                           (proj_b, T - 2), (agg_c_start, 0), (mul_w3, 0), (turn_w3, 1), (turn_b, T - 1), (mul_w3, 1),
                           (proj_b, T - 1)],
                     extra=[(turn_w3, 0), (turn_w3, 1), (agg_c_start, 0), (mul_w3, 0), (mul_w3, 1)])

            def proj_d(ph, l):
                def stage(i, p):
                    pe.wait_ge(ph.xT_ready.sem, ph.xT_ready.done(i + 1))
                    pe.wait_ge(ph.proj_ready.sem, ph.proj_ready.room(i))
                    for k in range(KD):
                        last = nc.tensor.matmul(bank(7, 0, D), xTs[:, p, k, :], W3[:, l, k, 0:D], start=(k == 0), stop=(k == KD - 1))
                    last.then_inc(ph.proj_done.sem, 1)
                return stage

            class scores:

                def __init__(self, g, l, ph, before):
                    self.g, self.l, self.ph, self.before = g, l, ph, before

                def mul_q(self, i, b):
                    for m in range(KD):
                        for k in range(KD):
                            last = nc.tensor.matmul(bank(b, m * P, (m + 1) * P), M3[:, self.l, k, m * P:(m + 1) * P],
                                                    xT[self.l][:, k, bass.ds(i * P, P)], start=(k == 0), stop=(k == KD - 1))
                    last.then_inc(self.g.q_done.sem, 1)

                def q_start(self, i, p):
                    pe.wait_ge(m3_ready.sem, 2)
                    pe.wait_ge(self.ph.xT_ready.sem, self.ph.xT_ready.done(1))
                    if self.before is not None:
                        pe.wait_ge(self.before.probs_ready.sem, self.before.probs_ready.done(T))
                    self.mul_q(0, 2)

                def q(self, i, p):
                    if isinstance(i, int) and i == 0:
                        return
                    pe.wait_ge(self.ph.proj_ready.sem, self.ph.proj_ready.done(T))
                    if self.l == 0 and not (isinstance(i, int) and i < 4):
                        pe.wait_ge(D1.proj_ready.sem, D1.proj_ready.done(i - 3))
                    self.mul_q(i, 7)

                def chunk(self, b, i, p):
                    c0, c1 = CH[b]
                    for k in range(KD):
                        last = nc.tensor.matmul(bank(b, 0, c1 - c0), Qs[:, p, k, :], xT[self.l][:, k, c0:c1],
                                                start=(k == 0), stop=(k == KD - 1))
                    return last

                def start(self, b, _):
                    if b == 0:
                        pe.wait_ge(self.g.Qs_ready.sem, 1)
                    pe.wait_ge(self.ph.xT_ready.sem, self.ph.xT_ready.done(min(-(-CH[b][1] // P), T)))
                    last = self.chunk(b, 0, 0)
                    if b == len(CH) - 1:
                        last.then_inc(self.g.scores_done.sem, 1)

                def __call__(self, i, p):
                    if isinstance(i, int) and i == 0:
                        return
                    pe.wait_ge(self.g.Qs_ready.sem, i + 1)
                    pe.wait_ge(self.g.probs_ready.sem, self.g.probs_ready.room(i))
                    for b in range(len(CH)):
                        last = self.chunk(b, i, p)
                    last.then_inc(self.g.scores_done.sem, 1)

            turn_xc, proj_c = turn_x(C, 5), proj_d(C, 0)
            s1 = scores(G[0], 0, C, None)
            pipeline(pe, T, [(turn_xc, 3), (agg_c, 1), (proj_c, 3)],
                     tail=[(turn_xc, T - 3), (agg_c, T - 1), (proj_c, T - 3), (turn_xc, T - 2), (s1.q_start, 0), (s1.start, 0),
                           (s1.start, 1), (turn_xc, T - 1), (proj_c, T - 2), (s1.start, 2), (proj_c, T - 1)],
                     extra=[(s1.q_start, 0), (s1.start, 0), (s1.start, 1), (s1.start, 2)])

            def turn_probs(g):
                def stage(i, p):
                    pe.wait_ge(pads_zero.sem, 2)
                    pe.wait_ge(g.probs_ready.sem, g.probs_ready.done(i + 1))
                    pe.wait_ge(g.probsT_ready.sem, g.probsT_ready.room(i))
                    for k in range(T):
                        last = nc.tensor.transpose(bank(3 + k // EB, (k % EB) * P, (k % EB) * P + P),
                                                   probs[:, p, k * P:(k + 1) * P], ident[:, :])
                    last.then_inc(g.turned.sem, 1)
                return stage

            def agg_d(ph, g, wh):
                def stage(i, p):
                    last_tile = isinstance(i, int) and i == T - 1
                    if not last_tile:
                        pe.wait_ge(g.probsT_ready.sem, g.probsT_ready.done(i + 1))
                    pe.wait_ge(ph.acc_read.sem, i + 2)
                    for k in range(T):
                        if last_tile and k % EB == 0:
                            pe.wait_ge(g.last_bank.sem, k // EB + 1)
                        last = nc.tensor.matmul(bank(6, 0, D), probsT[0:kk(k), p, k, :], wh[0:kk(k), k, :],
                                                start=(k == 0), stop=(k == T - 1))
                    last.then_inc(ph.agg_done.sem, 1)
                return stage

            def turned_bank_free(i):
                if isinstance(i, int) and i + 3 >= T:
                    pe.wait_ge(D1.proj_ready.sem, D1.proj_ready.done(i))
                else:
                    pe.wait_ge(G[0].Qs_ready.sem, i + 4)

            turn_xd, proj_d1 = turn_x(D1, 7, turned_bank_free), proj_d(D1, 1)
            turn_p1, agg_d1 = turn_probs(G[0]), agg_d(D1, G[0], Wh[0])
            s2 = scores(G[1], 1, D1, G[0])
            pipeline(pe, T, [(s1.q, 0), (turn_p1, 1), (turn_xd, 3), (s1, 0), (proj_d1, 3), (agg_d1, 1)],
                     tail=[(turn_p1, T - 1), (turn_xd, T - 3), (s2.q_start, 0), (proj_d1, T - 3), (s2.start, 0), (turn_xd, T - 2),
                           (agg_d1, T - 1), (s2.start, 1), (proj_d1, T - 2), (turn_xd, T - 1), (s2.start, 2), (proj_d1, T - 1)],
                     extra=[(s2.q_start, 0), (s2.start, 0), (s2.start, 1), (s2.start, 2)])
            pipeline(pe, T, [(s2.q, 0), (turn_probs(G[1]), 1), (s2, 0), (agg_d(D2, G[1], Wh[1]), 1)])


_INS = ['x', 'adj', 'L0_gnn_weight', 'L1_gnn_W_sa', 'L1_gnn_a_sa', 'L1_gnn_W_gcnb', 'L1_gnn_b_gcnb', 'L1_gnn_Wa',
        'L1_gnn_ba', 'L1_gnn_Wb', 'L1_gnn_bb', 'L2_gnn_W', 'L2_gnn_b', 'L3_gnn_W_stack']


def kernel(**inputs):
    import numpy as _np
    import concourse.bacc as _bacc
    from concourse import mybir as _mybir
    from concourse.bass_utils import run_bass_kernel_spmd as _run

    nc = _bacc.Bacc("TRN2", target_bir_lowering=False, num_devices=1)
    arrays, args = {}, []
    for name in _INS:
        a = _np.ascontiguousarray(inputs[name])
        arrays[f"in_{name}_dram"] = a
        args.append(nc.dram_tensor(f"in_{name}_dram", a.shape, _mybir.dt.from_np(a.dtype), kind="ExternalInput").ap())
    out = nc.dram_tensor("out_0_dram", inputs["x"].shape, _mybir.dt.float32, kind="ExternalOutput").ap()
    gnn_stack(nc, *args, out)
    r = _run(nc, [arrays], core_ids=[0])
    return r.results[0]["out_0_dram"]
```
